# Optimizing a Trainium2 kernel written in Bass

```python
import numpy as np
import jax
import jax.numpy as jnp

def _softmax(x, axis=-1):
    return jax.nn.softmax(x, axis=axis)

def _gelu(x):
    return jax.nn.gelu(x, approximate=True)

def _silu(x):
    return jax.nn.silu(x)

def _sigmoid(x):
    return jax.nn.sigmoid(x)

def _layernorm(x, axis=-1, eps=1e-05):
    m = jnp.mean(x, axis=axis, keepdims=True)
    v = jnp.var(x, axis=axis, keepdims=True)
    return (x - m) / jnp.sqrt(v + eps)

def _scatter_add(tgt, idx, src, axis=0):
    return tgt.at[idx].add(src)

def _segment_sum(src, seg, n):
    return jax.ops.segment_sum(src, seg, n)
kernel_name = 'mk_xattn_seq_d1_seqx_r2_40f633'

def setup_inputs(seed: int=0):
    np.random.seed(seed)
    _w = jnp.asarray

    def _rec_inputs():
        import jax
        import jax.numpy as jnp
        _rk = jax.random.key(seed)
        x = -0.000719 + 1.001 * jax.random.normal(jax.random.fold_in(_rk, 1), (2, 2048, 640), jnp.float32)
        _lenS = 2048 - jax.random.randint(jax.random.fold_in(_rk, 7), (2,), 0, max(1, 2048 // 4) + 1, jnp.int32)
        _lenS2 = 154 - jax.random.randint(jax.random.fold_in(_rk, 8), (2,), 0, max(1, 154 // 4) + 1, jnp.int32)
        _ctx_2048P = jax.random.normal(jax.random.fold_in(_rk, 11), (2, 16, 1024), jnp.float32)
        _ctx_2048c = jax.random.dirichlet(jax.random.fold_in(_rk, 511), 0.3 * jnp.ones((16,), jnp.float32), (2, 154))
        _ctx_2048t = jnp.einsum('bsk,bkd->bsd', _ctx_2048c, _ctx_2048P)
        _ctx_2048t = _ctx_2048t * jax.lax.rsqrt(jnp.mean(jnp.square(_ctx_2048t)) + 1e-12) * 0.953939
        ctx_2048 = 0.00257118 + 0.99863 * (_ctx_2048t + 0.3 * jax.random.normal(jax.random.fold_in(_rk, 611), (2, 154, 1024), jnp.float32))
        fside_S_0 = jax.random.uniform(jax.random.fold_in(_rk, 12), (2048,), jnp.float32, 0.0, 0.999706)
        return (x, ctx_2048, fside_S_0)
    x, ctx_2048, fside_S_0 = _rec_inputs()

    def _L0_xattn_setup():
        import jax, jax.numpy as jnp
        import numpy as np
        HEADS = 20
        NUM_TOKENS = 4
        IP_SCALE = 1.0
        SEM_SCALE = 0.5
        RESCALE = 1.0
        EPS = 1e-12

        def _l2norm(x, axis=-1):
            n = jnp.sqrt(jnp.sum(x * x, axis=axis, keepdims=True))
            return x / jnp.maximum(n, EPS)
        key = jax.random.key(seed)
        ks = jax.random.split(key, 10)
        B, S, C = (2, 512, 640)
        T, E = (81, 1024)
        inp = {'hidden_states': jax.random.normal(ks[0], (B, S, C), jnp.float32), 'encoder_hidden_states': jax.random.normal(ks[1], (B, T, E), jnp.float32), 'spatial_mask': jax.random.uniform(ks[2], (S,), jnp.float32), 'W_q': jax.random.normal(ks[3], (C, C), jnp.float32) * C ** (-0.5), 'W_k': jax.random.normal(ks[4], (E, C), jnp.float32) * E ** (-0.5), 'W_v': jax.random.normal(ks[5], (E, C), jnp.float32) * E ** (-0.5), 'W_k_ip': jax.random.normal(ks[6], (E, C), jnp.float32) * E ** (-0.5), 'W_v_ip': jax.random.normal(ks[7], (E, C), jnp.float32) * E ** (-0.5), 'W_out': jax.random.normal(ks[8], (C, C), jnp.float32) * C ** (-0.5), 'b_out': jnp.zeros((C,), jnp.float32)}
        return inp
    _L0_xattn_all = _L0_xattn_setup()
    _L0_xattn_in = {k: v for k, v in _L0_xattn_all.items() if k in ('W_q', 'W_k', 'W_v', 'W_k_ip', 'W_v_ip', 'W_out', 'b_out')}
    del _L0_xattn_all
    return {'x': x, 'ctx_2048': ctx_2048, 'fside_S_0': fside_S_0, 'L0_xattn_W_q': _L0_xattn_in['W_q'], 'L0_xattn_W_k': _L0_xattn_in['W_k'], 'L0_xattn_W_v': _L0_xattn_in['W_v'], 'L0_xattn_W_k_ip': _L0_xattn_in['W_k_ip'], 'L0_xattn_W_v_ip': _L0_xattn_in['W_v_ip'], 'L0_xattn_W_out': _L0_xattn_in['W_out'], 'L0_xattn_b_out': _L0_xattn_in['b_out']}

def reference(x, ctx_2048, fside_S_0, L0_xattn_W_q, L0_xattn_W_k, L0_xattn_W_v, L0_xattn_W_k_ip, L0_xattn_W_v_ip, L0_xattn_W_out, L0_xattn_b_out):
    import jax
    import jax.numpy as jnp

    def _L0_xattn_ref(hidden_states, encoder_hidden_states, spatial_mask, W_q, W_k, W_v, W_k_ip, W_v_ip, W_out, b_out):
        import jax, jax.numpy as jnp
        import numpy as np
        HEADS = 20
        NUM_TOKENS = 4
        IP_SCALE = 1.0
        SEM_SCALE = 0.5
        RESCALE = 1.0
        EPS = 1e-12

        def _l2norm(x, axis=-1):
            n = jnp.sqrt(jnp.sum(x * x, axis=axis, keepdims=True))
            return x / jnp.maximum(n, EPS)
        B, S, C = hidden_states.shape
        H = HEADS
        Dh = C // H
        attn_scale = Dh ** (-0.5)
        residual = hidden_states
        text_ehs = encoder_hidden_states[:, :-NUM_TOKENS]
        ip_ehs = encoder_hidden_states[:, -NUM_TOKENS:]

        def heads(x):
            return x.reshape(B, -1, H, Dh).transpose(0, 2, 1, 3)
        q = heads(hidden_states @ W_q)
        k_t = heads(text_ehs @ W_k)
        v_t = heads(text_ehs @ W_v)
        scores_t = jnp.einsum('bhsd,bhtd->bhst', q, k_t) * attn_scale
        probs_t = jax.nn.softmax(scores_t, axis=-1)
        text_out = jnp.einsum('bhst,bhtd->bhsd', probs_t, v_t)
        text_out = text_out.transpose(0, 2, 1, 3).reshape(B, S, C)
        k_ip = heads(ip_ehs @ W_k_ip)
        v_ip = heads(ip_ehs @ W_v_ip)
        attn_scores = jnp.einsum('bhsd,bhnd->bhsn', q, k_ip) * attn_scale
        qsem = jnp.einsum('bhst,bte->bhse', probs_t, text_ehs)
        qsem = _l2norm(qsem)
        ip_n = _l2norm(ip_ehs)
        sem = jnp.einsum('bhse,bne->bhsn', qsem, ip_n)
        sem = jax.lax.stop_gradient(sem)
        fused = attn_scores + SEM_SCALE * sem
        probs_ip = jax.nn.softmax(fused, axis=-1)
        probs_ip = probs_ip * spatial_mask[None, None, :, None]
        ip_out = jnp.einsum('bhsn,bhnd->bhsd', probs_ip, v_ip)
        ip_out = ip_out.transpose(0, 2, 1, 3).reshape(B, S, C)
        out = text_out + IP_SCALE * ip_out
        out = out @ W_out + b_out
        out = out + residual
        return out / RESCALE
    x = _L0_xattn_ref(x, ctx_2048, fside_S_0, L0_xattn_W_q, L0_xattn_W_k, L0_xattn_W_v, L0_xattn_W_k_ip, L0_xattn_W_v_ip, L0_xattn_W_out, L0_xattn_b_out)
    return x

_drawn_inputs = setup_inputs


def setup_inputs(seed=0):
    import zlib

    import numpy as np

    out = dict(_drawn_inputs(seed))
    spreads = {'L0_xattn_b_out': (0.0, 0.1)}
    factors = {}
    for name, (base, spread) in spreads.items():
        noise = np.random.default_rng([zlib.crc32(name.encode()), seed]).standard_normal(out[name].shape)
        drawn = base * np.exp(spread * noise) if base else spread * noise
        out[name] = jnp.asarray(drawn.astype(out[name].dtype))
    for name, factor in factors.items():
        out[name] = (out[name] * factor).astype(out[name].dtype)
    return out
```

```python
from contextlib import ExitStack

import concourse.bass as bass
from concourse import mybir

F32 = mybir.dt.float32
ACT = mybir.ActivationFunctionType
ALU = mybir.AluOpType
AX_X = mybir.AxisListType.X

P = 128
HEADS = 20
NIP = 4
EPS = 1e-12
SEM_SCALE = 0.5

BANK_B, BANK_T, BANK_N, BANK_M = 0, 2, 4, 6


def repeated(ap, axis, n):
    shape = list(ap.shape)
    shape[axis] = n
    return ap.broadcast_to(shape)


def xattn_program(nc, x, ctx, mask, w_q, w_k, w_v, w_k_ip, w_v_ip, w_out, b_out, out):
    B, S, C = x.shape
    TA, E = ctx.shape[1:]
    T = TA - NIP
    TR = T - P
    D = C // HEADS
    SCALE = float(D) ** -0.5
    CC = C // P
    EC = E // P
    HG = P // D
    NG = HEADS // HG
    U = 4
    NST = B * S // (U * P)
    SPB = NST // B
    TPB = S // P
    HALF = C // 2
    LG = U * NG
    W = D + NIP + 1 + T
    W_A, W_Z, W_G = D, D + NIP, D + NIP + 1
    WR = W_G + TR
    assert D == 32 and NG == CC and 0 < TR <= D and TA * 2 <= 512 and W * 2 <= 512 and LG % 2 == 0

    C_REST = B * P
    C_IP = C_REST + B * 32
    C_IPN = C_IP + B * NIP
    C_ALL = C_IPN + B * NIP

    x_t = x.rearrange("b (t p) c -> (b t) p c", p=P)
    out_t = out.rearrange("b (t p) c -> (b t) p c", p=P)

    with ExitStack() as stack:
        def sb(name, shape, dt=F32):
            return stack.enter_context(nc.sbuf_tensor(name, shape, dt))

        def sem(name):
            return stack.enter_context(nc.semaphore(name))

        ps = stack.enter_context(nc.psum_tensor("ps", [P, 8, 512], F32))

        ident = sb("ident", [P, P])
        area = sb("area", [P, 11000])
        cut = [0]

        def part(rows, *dims):
            n = 1
            for d in dims:
                n *= d
            view = area[0:rows, cut[0]:cut[0] + n]
            cut[0] += n
            if len(dims) == 1:
                return view
            names = "abc"[:len(dims)]
            return view.rearrange(f"p ({' '.join(names)}) -> p {' '.join(names)}",
                                  **dict(zip(names[1:], dims[1:])))

        ctx_main = part(P, B, E)
        ctx_rest = part(B * 32, E)
        ip_raw = part(B * NIP, E)
        ip_nrm = part(B * NIP, E)
        ctxT = part(P, EC, C_ALL)
        mask_rows = part(TPB, P)
        v_rest = part(B * 32, C)
        g_rest = part(B * 32, WR - D)
        vip_blk = part(P, B, CC * (HEADS * NIP // CC + HEADS * NIP))
        ip_sq = sb("ip_sq", [B * NIP, 1])
        ip_sqg = sb("ip_sqg", [B * NIP, 1])
        ip_rn = sb("ip_rn", [B * NIP, 1])
        minus_half = sb("minus_half", [P, HEADS])
        w_stage = sb("w_stage", [P, 2, EC, C])
        wq_sb = sb("wq_sb", [P, CC, C])
        wo_sb = sb("wo_sb", [P, CC, C])
        mask_sb = sb("mask_sb", [P, TPB])
        bias_sb = sb("bias_sb", [P, C])
        wv = sb("wv", [HEADS * NIP, B, C])
        k_tab = sb("k_tab", [P, B, HEADS // 2, 2 * TA])
        t_main = sb("t_main", [P, B, HEADS, W])
        t_rest = sb("t_rest", [P, B, NG, HG, WR])

        x_in = sb("x_in", [P, 2, C])
        xT = sb("xT", [P, CC, U * P])
        q_next = sb("q_next", [P, CC, U * P])
        cut[0] = 0
        neg_max = part(P, 2, HG)
        e = part(P, 2, HG, T)
        e_rest = part(P, HG, 32)
        eT = part(P, HG, P)
        eT_rest = part(P, P)
        stats = part(P, 2, HEADS, W_G)
        text = part(P, HEADS, D)
        oT = part(P, CC + 1, P)
        x_res = part(P, 2, C)
        y = part(P, 2, C)
        q_cur = part(P, U, CC, P)
        ege = part(P, 2, HEADS)
        ip_score = part(P, 2, HEADS, NIP)
        z_inv = part(P, HEADS)
        z_sq = part(P, HEADS)
        n_sq = part(P, HEADS)
        n_inv = part(P, HEADS)
        sem_raw = part(P, HEADS, NIP)
        fused = part(P, HEADS, NIP)
        f_min = part(P, HEADS)
        f_diff = part(P, HEADS, NIP)
        e_ip = part(P, HEADS, NIP)
        ip_sum = part(P, HEADS)
        ip_inv = part(P, HEADS)
        ip_w = part(P, HEADS)
        p_ip = part(P, HEADS, NIP)

        ld_ctx, ld_ip, ld_k, ld_v, ld_kip, ld_vip, ld_q, ld_out, ld_small = (
            sem(f"ld_{n}") for n in ("ctx", "ip", "k", "v", "kip", "vip", "q", "out", "small"))
        ident_ready, zeroed, half_ready = sem("ident_ready"), sem("zeroed"), sem("half_ready")
        ident_zero, ip_sq_ready, ip_guard, ip_rn_ready, ip_nrm_ready = (
            sem(n) for n in ("ident_zero", "ip_sq_ready", "ip_guard", "ip_rn_ready", "ip_nrm_ready"))
        job_done, job_act, job_dve = sem("job_done"), sem("job_act"), sem("job_dve")
        rest_staged, rest_tab, vip_ready, wv_ready = (
            sem(n) for n in ("rest_staged", "rest_tab", "vip_ready", "wv_ready"))
        ld_x = [sem("ld_x0"), sem("ld_x1")]
        xT_psum, xT_ready = sem("xT_psum"), sem("xT_ready")
        q_psum, q_evac, q_ready = sem("q_psum"), sem("q_evac"), sem("q_ready")
        scores, max_ready, e_ready = sem("scores"), sem("max_ready"), sem("e_ready")
        eT_psum, eT_ready, prod, stats_ready, dots = (
            sem(n) for n in ("eT_psum", "eT_ready", "prod", "stats_ready", "dots"))
        z_ready, text_ready, nsq_ready, ninv_ready, chain = (
            sem(n) for n in ("z_ready", "text_ready", "nsq_ready", "ninv_ready", "chain"))
        diff_ready, eip_ready, ipw_ready, pip_ready = (
            sem(n) for n in ("diff_ready", "eip_ready", "ipw_ready", "pip_ready"))
        rest_ready = sem("rest_ready")
        oT_psum, oT_ready, y_psum, y_ready = (
            sem(n) for n in ("oT_psum", "oT_ready", "y_psum", "y_ready"))
        ld_res = [sem("ld_res0"), sem("ld_res1")]
        res_ready = sem("res_ready")
        st_y = [sem("st_y0"), sem("st_y1")]

        block = stack.enter_context(nc.Block())

        jobs = [("ctxT", c, 0) for c in range(EC)]
        jobs += [("kT", g, 0) for g in range(NG)]
        jobs += [("g", b, 0) for b in range(B)] + [("g_rest", 0, 0), ("mask", 0, 0)]
        jobs += [("v", b, h) for b in range(B) for h in range(2)]
        jobs += [("v_rest", h, 0) for h in range(2)]
        jobs += [("kip", 0, 0), ("vip", 0, 0)]
        jobs += [("wv", b, h) for b in range(B) for h in range(2)]

        def job_at(kind):
            return [k for k, j in enumerate(jobs) if j[0] == kind]

        def emptied(eng, k):
            if k % 2 == 0:
                eng.wait_ge(job_act, k // 2 + 1)
            else:
                eng.wait_ge(job_dve, k // 2 + 1)

        def prepared(eng):
            eng.wait_ge(job_done, len(jobs))
            eng.wait_ge(job_act, (len(jobs) + 1) // 2)
            eng.wait_ge(job_dve, len(jobs) // 2)
            eng.wait_ge(rest_tab, 1)

        SEGMENTS = []
        for b in range(B):
            lo, hi = b * SPB, (b + 1) * SPB
            SEGMENTS.append((lo, lo + 1, b))
            top = hi - 1 if b == B - 1 else hi
            if top > lo + 1:
                SEGMENTS.append((lo + 1, top, b))
            if b == B - 1:
                SEGMENTS.append((hi - 1, hi, b))

        def supertiles(eng):
            for lo, hi, b in SEGMENTS:
                if hi - lo == 1:
                    yield lo, b
                else:
                    with eng.Fori(lo, hi) as st:
                        yield st, b

        def is_at(st, v):
            return isinstance(st, int) and st == v

        LAST = NST - 1
        SPARE = {(1, 0): ("xT", 0), (1, 1): ("xT", 1), (1, 2): ("xT", 2), (2, 0): ("xT", 3),
                 (2, 1): ("q", 0), (2, 2): ("q", 1), (3, 0): ("q", 2), (3, 1): ("q", 3),
                 (3, 2): ("q", 4)}
        for u in range(U):
            SPARE[(u, 3)] = ("oT", 0)
            SPARE[(u, 4)] = ("y", 0)
        assert CC == 5 and NG == 5

        def spare(st, u, g):
            work = SPARE.get((u, g))
            if work is None or (work[0] in ("xT", "q") and is_at(st, LAST)):
                return None
            if work[0] in ("oT", "y") and is_at(st, 0) and u == 0:
                return None
            return work

        @block.sync
        def _(sp):
            for b in range(B):
                sp.dma_start(ctx_main[:, b, :], ctx[b, TR:T, :]).then_inc(ld_ctx, 16)
                sp.dma_start(ctx_rest[b * 32:b * 32 + 32, :], ctx[b, 0:32, :]).then_inc(ld_ctx, 16)
                sp.dma_start(ip_raw[b * NIP:(b + 1) * NIP, :], ctx[b, T:TA, :]).then_inc(ld_ip, 16)
            sp.dma_start(w_stage[:, 0], w_k.rearrange("(c p) n -> p c n", p=P)).then_inc(ld_k, 16)
            sp.dma_start(w_stage[:, 1], w_v.rearrange("(c p) n -> p c n", p=P)).then_inc(ld_v, 16)
            def load_x(s, k):
                if not (is_at(s, 0) and k < 2):
                    sp.wait_ge(xT_psum, s * U + k - 1)
                sp.dma_start(x_in[:, k % 2, :], x_t[s * U + k]).then_inc(ld_x[k % 2], 16)

            load_x(0, 0)
            load_x(0, 1)
            sp.dma_start(wq_sb[:], w_q.rearrange("(c p) n -> p c n", p=P)).then_inc(ld_q, 16)
            sp.dma_start(wo_sb[:], w_out.rearrange("(c p) n -> p c n", p=P)).then_inc(ld_out, 16)
            sp.dma_start(mask_rows[:], mask.rearrange("(t p) -> t p", p=P)).then_inc(ld_small, 16)
            sp.dma_start(bias_sb[:], repeated(b_out.rearrange("(a n) -> a n", a=1), 0, P)).then_inc(ld_small, 16)
            sp.wait_ge(job_done, job_at("kT")[-1] + 1)
            sp.dma_start(w_stage[:, 0], w_k_ip.rearrange("(c p) n -> p c n", p=P)).then_inc(ld_kip, 16)
            load_x(0, 2)
            load_x(0, 3)
            sp.wait_ge(job_done, job_at("v_rest")[-1] + 1)
            sp.dma_start(w_stage[:, 1], w_v_ip.rearrange("(c p) n -> p c n", p=P)).then_inc(ld_vip, 16)
            prepared(sp)
            for st, _b in supertiles(sp):
                for u in range(U):
                    tile = st * U + u
                    if not (is_at(st, 0) and u < 2):
                        sp.wait_ge(y_ready, tile - 1)
                    sp.dma_start(x_res[:, u % 2, :], x_t[tile]).then_inc(ld_res[u % 2], 16)
                    if u < 2 and not is_at(st, LAST):
                        load_x(st + 1, 2 * u)
                        load_x(st + 1, 2 * u + 1)
                    if not (is_at(st, 0) and u == 0):
                        sp.wait_ge(y_ready, tile)
                        sp.dma_start(out_t[tile - 1], y[:, (u + 1) % 2, :]
                                     ).then_inc(st_y[(u + 1) % 2], 16)
            sp.wait_ge(y_ready, NST * U)
            sp.dma_start(out_t[NST * U - 1], y[:, 1, :]).then_inc(st_y[1], 16)
            for k in range(2):
                sp.wait_ge(st_y[k], 16 * NST * U // 2)

        def norm_tail(pool, tile, par):
            pool.wait_ge(nsq_ready, tile + 1)
            nc.gpsimd.tensor_tensor(n_inv[:], n_sq[:], minus_half[:], ALU.pow).then_inc(ninv_ready, 1)
            pool.wait_ge(z_ready, tile + 1)
            if not is_at(tile, 0):
                pool.wait_ge(oT_psum, tile)
            nc.gpsimd.tensor_tensor(text[:], stats[:, par, :, 0:D],
                                    repeated(z_inv[:].rearrange("p (h a) -> p h a", a=1), 2, D), ALU.mult
                                    ).then_inc(text_ready, 1)

        @block.gpsimd
        def _(pool):
            nc.gpsimd.memset(ident[:], 0.0).then_inc(ident_zero, 1)
            pool.wait_ge(ident_zero, 1)
            nc.gpsimd.affine_select(out=ident[:], in_=ident[:], compare_op=ALU.not_equal, fill=1.0,
                                    base=0, pattern=[[-1, P]], channel_multiplier=1
                                    ).then_inc(ident_ready, 1)
            nc.gpsimd.memset(minus_half[:], -0.5).then_inc(half_ready, 1)
            nc.gpsimd.memset(k_tab[:], 0.0).then_inc(zeroed, 1)
            pool.wait_ge(ip_guard, 1)
            pool.wait_ge(half_ready, 1)
            nc.gpsimd.tensor_tensor(ip_rn[:], ip_sqg[:], minus_half[0:B * NIP, 0:1], ALU.pow
                                    ).then_inc(ip_rn_ready, 1)
            nc.gpsimd.memset(t_rest[:], 0.0).then_inc(zeroed, 1)
            nc.gpsimd.memset(vip_blk[:], 0.0).then_inc(zeroed, 1)
            nc.gpsimd.memset(t_main[:, :, :, W_Z:W_Z + 1], 1.0).then_inc(zeroed, 1)
            nc.gpsimd.memset(g_rest[:, NIP:NIP + 1], 1.0).then_inc(rest_staged, 1)
            pool.wait_ge(ld_small, 32)

            prepared(pool)
            for st, _b in supertiles(pool):
                for u in range(U):
                    tile = st * U + u
                    pool.wait_ge(ld_res[u % 2], (st * (U // 2) + u // 2 + 1) * 16)
                    nc.gpsimd.tensor_tensor(x_res[:, u % 2, :], x_res[:, u % 2, :], bias_sb[:], ALU.add
                                            ).then_inc(res_ready, 1)
                    if not (is_at(st, 0) and u == 0):
                        norm_tail(pool, tile - 1, (u + 1) % 2)
            norm_tail(pool, NST * U - 1, 1)

        def empty(eng, k, cp):
            kind, a, h = jobs[k]
            bank = ps[:, k % 4, :]
            if kind == "ctxT":
                return cp(ctxT[:, a, :], bank[:, 0:C_ALL])
            if kind == "kT":
                for b in range(B):
                    for j in range(HG):
                        q = slice(D * j, D * j + D)
                        dst = k_tab[q, b, 2 * a + j // 2, (j % 2) * TA:(j % 2) * TA + T]
                        cp(dst[:, 0:TR], bank[q, C_REST + 32 * b:C_REST + 32 * b + TR], -SCALE)
                        last = cp(dst[:, TR:T], bank[q, P * b:P * b + P], -SCALE)
                return last
            if kind == "g":
                def all_heads(lo, n):
                    return repeated(bank[:, lo:lo + n].rearrange("p (a n) -> p a n", a=1), 1, HEADS)
                cp(t_main[:, a, :, W_A:W_Z], all_heads(C_IPN + NIP * a, NIP))
                cp(t_main[:, a, :, W_G:WR], all_heads(C_REST + 32 * a, TR), 2.0)
                return cp(t_main[:, a, :, WR:W], all_heads(P * a, P))
            if kind == "g_rest":
                for b in range(B):
                    r = slice(32 * b, 32 * b + 32)
                    lo = C_IPN - C_REST + NIP * b
                    cp(g_rest[r, 0:NIP], bank[r, lo:lo + NIP])
                    last = cp(g_rest[r, NIP + 1:], bank[r, 32 * b:32 * b + TR])
                return last
            if kind == "mask":
                return cp(mask_sb[:], bank[:, 0:TPB])
            if kind == "v":
                return cp(t_main[:, a, h * 10:h * 10 + 10, 0:D],
                          bank[:, 0:HALF].rearrange("p (n d) -> p n d", d=D))
            if kind == "v_rest":
                return cp(v_rest[:, a * HALF:(a + 1) * HALF], bank[0:B * 32, 0:HALF])
            if kind == "kip":
                for b in range(B):
                    for j in range(HG):
                        q = slice(D * j, D * j + D)
                        lo = (j % 2) * TA + T
                        dst = k_tab[q, b, j // 2:HEADS // 2:2, lo:lo + NIP]
                        src = bank[q, 0:CC * B * NIP].rearrange("p (g n) -> p g n", g=CC)
                        last = cp(dst, src[:, :, b * NIP:(b + 1) * NIP], -SCALE)
                return last
            if kind == "vip":
                step = HEADS * NIP + HG * NIP
                for b in range(B):
                    for j in range(HG):
                        q = slice(D * j, D * j + D)
                        dst = vip_blk[q, b, :].rearrange("p (g r) -> p g r", r=step)
                        src = bank[q, 0:CC * B * NIP].rearrange("p (g n) -> p g n", g=CC)
                        last = cp(dst[:, :, j * NIP:(j + 1) * NIP], src[:, :, b * NIP:(b + 1) * NIP])
                return last
            assert kind == "wv"
            return cp(wv[:, a, h * HALF:(h + 1) * HALF], bank[0:HEADS * NIP, 0:HALF])

        @block.scalar
        def _(act):
            def cp(o, i, scale=1.0):
                return nc.scalar.activation(o, i, ACT.Copy, scale=scale)

            def evac_x(s, k):
                act.wait_ge(xT_psum, s * U + k + 1)
                if k == 0 and not is_at(s, 0):
                    act.wait_ge(q_psum, s * CC)
                cols = slice(k * P, (k + 1) * P)
                nc.scalar.activation(xT[:, 0:4, cols],
                                     ps[:, BANK_M, :].rearrange("p (c s) -> p c s", c=4), ACT.Copy)
                nc.scalar.activation(xT[:, 4, cols], ps[:, BANK_M + 1, 0:P], ACT.Copy
                                     ).then_inc(xT_ready, 1)

            def evac_q(s, k):
                act.wait_ge(q_psum, s * CC + k + 1)
                if k == 0 and not is_at(s, 0):
                    act.wait_ge(q_ready, s * U)
                nc.scalar.activation(q_next[:, k, :], ps[:, BANK_M + k % 2, :], ACT.Copy
                                     ).then_inc(q_evac, 1)

            def evac_eT(i, par):
                act.wait_ge(eT_psum, i + 1)
                nc.scalar.activation(eT[:], ps[:, BANK_T, :].rearrange("p (h s) -> p h s", h=HG), ACT.Copy)
                nc.scalar.activation(eT_rest[:], ps[:, BANK_T + 1, 0:P], ACT.Copy).then_inc(eT_ready, 1)

            def copy_stats(i, g, tpar):
                act.wait_ge(prod, i + 1)
                src = ps[:, BANK_N:BANK_N + 2, 0:2 * W].rearrange("p b (h w) -> p b h w", h=2)
                dst = stats[:, tpar, g * HG:(g + 1) * HG, :].rearrange("p (b h) w -> p b h w", b=2)
                nc.scalar.activation(dst, src[:, :, :, 0:W_G], ACT.Copy).then_inc(stats_ready, 1)

            def exp_ip(tile):
                act.wait_ge(diff_ready, tile + 1)
                nc.scalar.activation(e_ip[:], f_diff[:], ACT.Exp).then_inc(eip_ready, 1)

            def evac_oT(tile):
                act.wait_ge(oT_psum, tile + 1)
                if not is_at(tile, 0):
                    act.wait_ge(y_psum, tile)
                nc.scalar.activation(oT[:, 0:4, :],
                                     ps[:, BANK_M, :].rearrange("p (c s) -> p c s", c=4), ACT.Copy)
                nc.scalar.activation(oT[:, 4, :], ps[:, BANK_M + 1, 0:P], ACT.Copy)
                nc.scalar.activation(oT[0:HEADS * NIP, 5, :], ps[0:HEADS * NIP, BANK_M + 1, P:2 * P],
                                     ACT.Copy).then_inc(oT_ready, 1)

            zeros_needed = {"kT": 1, "kip": 1, "vip": 3}
            for k in range(0, len(jobs), 2):
                if k == job_at("kip")[0] + 1:
                    for t in range(U):
                        evac_x(0, t)
                    for t in range(CC):
                        evac_q(0, t)
                act.wait_ge(job_done, k + 1)
                if jobs[k][0] in zeros_needed:
                    act.wait_ge(zeroed, zeros_needed[jobs[k][0]])
                empty(act, k, cp).then_inc(job_act, 1)

            prepared(act)
            for st, _b in supertiles(act):
                for u in range(U):
                    for g in range(NG):
                        i = st * LG + u * NG + g
                        par = (u * NG + g) % 2
                        first = is_at(st, 0) and u == 0 and g == 0
                        if not first:
                            evac_eT(i - 1, 1 - par)
                        act.wait_ge(max_ready, i + 1)
                        if not (is_at(st, 0) and u == 0 and g < 2):
                            act.wait_ge(dots, i - 1)
                        for j in range(HG):
                            src = ps[:, BANK_B + j // 2, (j % 2) * TA:(j % 2) * TA + T]
                            last = nc.scalar.activation(e[:, par, j, :], src, ACT.Exp,
                                                        bias=neg_max[:, par, j:j + 1], scale=-1.0)
                        last.then_inc(e_ready, 1)
                        if not first:
                            pg, pt = (g - 1) % NG, (u if g else u + 1) % 2
                            copy_stats(i - 1, pg, pt)
                        tile = st * U + u
                        if g == 1 and not (is_at(st, 0) and u == 0):
                            exp_ip(tile - 1)
                        work = spare(st, u, g)
                        if work and work[0] == "xT":
                            evac_x(st + 1, work[1])
                        elif work and work[0] == "q":
                            evac_q(st + 1, work[1])
                        elif work and work[0] == "oT":
                            evac_oT(tile - 1)
            evac_eT(NST * LG - 1, 1)
            copy_stats(NST * LG - 1, NG - 1, 1)
            exp_ip(NST * U - 1)
            evac_oT(NST * U - 1)

        @block.vector
        def _(dve):
            def cp(o, i, scale=1.0):
                if scale == 1.0:
                    return nc.vector.tensor_copy(o, i)
                return nc.vector.tensor_scalar(o, i, scale, None, ALU.mult)

            dve.wait_ge(ld_ip, 16 * B)
            nc.vector.tensor_tensor_reduce(out=ip_nrm[:], in0=ip_raw[:], in1=ip_raw[:], scale=1.0,
                                           scalar=0.0, op0=ALU.mult, op1=ALU.add,
                                           accum_out=ip_sq[:]).then_inc(ip_sq_ready, 1)
            dve.wait_ge(ip_sq_ready, 1)
            nc.vector.tensor_scalar(ip_sqg[:], ip_sq[:], EPS * EPS, None, ALU.max).then_inc(ip_guard, 1)
            dve.wait_ge(ip_rn_ready, 1)
            nc.vector.tensor_scalar(ip_nrm[:], ip_raw[:], ip_rn[:], None, ALU.mult
                                    ).then_inc(ip_nrm_ready, 1)
            zeros_needed = {"kT": 1, "kip": 1, "vip": 3}
            for k in range(1, len(jobs), 2):
                dve.wait_ge(job_done, k + 1)
                if jobs[k][0] in zeros_needed:
                    dve.wait_ge(zeroed, zeros_needed[jobs[k][0]])
                empty(dve, k, cp).then_inc(job_dve, 1)
                if k == job_at("kip")[0]:
                    emptied(dve, job_at("g_rest")[0])
                    dve.wait_ge(zeroed, 4)
                    dve.wait_ge(rest_staged, 1)
                    for v in job_at("v_rest"):
                        emptied(dve, v)
                    for b in range(B):
                        for j in range(HG):
                            q = slice(D * j, D * j + TR)
                            r = slice(32 * b, 32 * b + TR)
                            nc.vector.tensor_copy(
                                t_rest[q, b, :, j, 0:D],
                                v_rest[r, :].rearrange("p (g h d) -> p g h d", h=HG, d=D)[:, :, j, :])
                            last = nc.vector.tensor_copy(
                                t_rest[q, b, :, j, D:WR],
                                repeated(g_rest[r, :].rearrange("p (a n) -> p a n", a=1), 1, NG))
                    last.then_inc(rest_tab, 1)

            def spread_q(u):
                nc.vector.tensor_copy(q_cur[:, u], q_next[:, :, u * P:(u + 1) * P]).then_inc(q_ready, 1)

            prepared(dve)
            dve.wait_ge(q_evac, CC)
            for u in range(U):
                spread_q(u)

            def tail_a(tile, par):
                dve.wait_ge(stats_ready, (tile + 1) * NG)
                if not is_at(tile, 0):
                    dve.wait_ge(text_ready, tile)
                z = stats[:, par, :, W_Z]
                nc.vector.reciprocal(z_inv[:], z).then_inc(z_ready, 1)
                nc.vector.tensor_tensor(z_sq[:], z, z, ALU.mult).then_inc(chain, 1)
                dve.wait_ge(chain, tile * CH + 1)
                dve.wait_ge(dots, (tile + 1) * NG)
                nc.vector.scalar_tensor_tensor(out=n_sq[:], in0=z_sq[:], scalar=EPS * EPS,
                                               in1=ege[:, par, :], op0=ALU.mult, op1=ALU.max
                                               ).then_inc(nsq_ready, 1)

            CH = 6

            def tail_b(tile, par):
                dve.wait_ge(ninv_ready, tile + 1)
                nc.vector.tensor_tensor(
                    sem_raw[:], stats[:, par, :, W_A:W_Z],
                    repeated(n_inv[:].rearrange("p (h a) -> p h a", a=1), 2, NIP), ALU.mult
                ).then_inc(chain, 1)
                dve.wait_ge(chain, tile * CH + 2)
                nc.vector.scalar_tensor_tensor(out=fused[:], in0=sem_raw[:], scalar=-SEM_SCALE,
                                               in1=ip_score[:, par], op0=ALU.mult, op1=ALU.add
                                               ).then_inc(chain, 1)
                dve.wait_ge(chain, tile * CH + 3)
                nc.vector.tensor_reduce(f_min[:], fused[:], axis=AX_X, op=ALU.min).then_inc(chain, 1)
                dve.wait_ge(chain, tile * CH + 4)
                nc.vector.tensor_tensor(
                    f_diff[:], repeated(f_min[:].rearrange("p (h a) -> p h a", a=1), 2, NIP), fused[:],
                    ALU.subtract).then_inc(diff_ready, 1)

            def tail_c(tile, col):
                dve.wait_ge(eip_ready, tile + 1)
                nc.vector.reduce_sum(ip_sum[:], e_ip[:], AX_X).then_inc(chain, 1)
                dve.wait_ge(chain, tile * CH + 5)
                nc.vector.reciprocal(ip_inv[:], ip_sum[:]).then_inc(chain, 1)
                dve.wait_ge(chain, tile * CH + 6)
                nc.vector.tensor_scalar(ip_w[:], ip_inv[:], mask_sb[:, col], None, ALU.mult
                                        ).then_inc(ipw_ready, 1)
                dve.wait_ge(ipw_ready, tile + 1)
                if not is_at(tile, 0):
                    dve.wait_ge(oT_psum, tile)
                nc.vector.tensor_tensor(
                    p_ip[:], e_ip[:], repeated(ip_w[:].rearrange("p (h a) -> p h a", a=1), 2, NIP),
                    ALU.mult).then_inc(pip_ready, 1)

            def add_residual(tile, par, stores):
                dve.wait_ge(y_psum, tile + 1)
                dve.wait_ge(res_ready, tile + 1)
                if stores is not None:
                    dve.wait_ge(st_y[par], stores)
                src = ps[:, BANK_M:BANK_M + 2, 0:HALF]
                nc.vector.tensor_tensor(y[:, par, :].rearrange("p (b n) -> p b n", b=2), src,
                                        x_res[:, par, :].rearrange("p (b n) -> p b n", b=2), ALU.add
                                        ).then_inc(y_ready, 1)

            def group_dots(i, g, par, tpar):
                dve.wait_ge(stats_ready, i + 1)
                for j in range(HG):
                    lo = (j % 2) * W + W_G
                    last = nc.vector.tensor_tensor_reduce(
                        out=e[:, par, j, :], in0=ps[:, BANK_N + j // 2, lo:lo + T], in1=e[:, par, j, :],
                        scale=1.0, scalar=0.0, op0=ALU.mult, op1=ALU.add,
                        accum_out=ege[:, tpar, g * HG + j:g * HG + j + 1])
                last.then_inc(dots, 1)

            for st, b in supertiles(dve):
                for u in range(U):
                    tile = st * U + u
                    for g in range(NG):
                        i = st * LG + u * NG + g
                        par = (u * NG + g) % 2
                        dve.wait_ge(scores, i + 1)
                        src = ps[:, BANK_B:BANK_B + 2, 0:2 * TA].rearrange("p b (h t) -> p b h t", h=2)
                        nc.vector.tensor_copy(
                            ip_score[:, u % 2, g * HG:(g + 1) * HG, :].rearrange("p (b h) n -> p b h n", b=2),
                            src[:, :, :, T:TA])
                        nc.vector.tensor_reduce(
                            neg_max[:, par, :].rearrange("p (b h) -> p b h", b=2),
                            src[:, :, :, 0:T], axis=AX_X, op=ALU.min).then_inc(max_ready, 1)
                        if not (is_at(st, 0) and u == 0 and g == 0):
                            group_dots(i - 1, (g - 1) % NG, 1 - par, (u if g else u + 1) % 2)
                        dve.wait_ge(e_ready, i + 1)
                        if not (is_at(st, 0) and u == 0 and g == 0):
                            dve.wait_ge(eT_psum, i)
                        nc.vector.tensor_copy(e_rest[:], e[:, par, :, 0:32]).then_inc(rest_ready, 1)
                        if is_at(st, 0) and u == 0:
                            continue
                        if g == 0:
                            tail_a(tile - 1, (u + 1) % 2)
                        elif g == 1:
                            tail_b(tile - 1, (u + 1) % 2)
                        elif g == 2:
                            within = (tile - 1) % TPB if isinstance(st, int) else tile - 1 - b * TPB
                            tail_c(tile - 1, bass.ds(within, 1))
                        elif g == 4:
                            if is_at(st, 0) and u < 3:
                                stores = None
                            else:
                                stores = (st * (U // 2) + (u - 1) // 2) * 16
                            add_residual(tile - 1, (u + 1) % 2, stores)
                        if u == U - 1 and g >= 3 and not is_at(st, LAST):
                            if g == 3:
                                dve.wait_ge(q_evac, (st + 2) * CC)
                            for k in ((0, 1, 2) if g == 3 else (3,)):
                                spread_q(k)
            n = NST * U - 1
            group_dots(NST * LG - 1, NG - 1, 1, 1)
            tail_a(n, 1)
            tail_b(n, 1)
            tail_c(n, bass.ds(TPB - 1, 1))
            add_residual(n, 1, (n // 2) * 16)

        @block.tensor
        def _(pe):
            pe.wait_ge(ident_ready, 1)
            pe.wait_ge(ld_ctx, 32 * B)

            def run_job(k):
                kind, a, h = jobs[k]
                bank = ps[:, k % 4, :]
                if k >= 4:
                    emptied(pe, k - 4)
                if kind == "ctxT":
                    if k == 0:
                        pe.wait_ge(ip_nrm_ready, 1)
                    cols = slice(a * P, (a + 1) * P)
                    parts = [(ctx_main[:, b, cols], P * b) for b in range(B)]
                    parts += [(ctx_rest[:, cols], C_REST), (ip_raw[:, cols], C_IP), (ip_nrm[:, cols], C_IPN)]
                    for src, lo in parts:
                        n = src.shape[0]
                        last = nc.tensor.transpose(bank[:, lo:lo + n], src, ident[0:n, 0:n])
                    return last
                if kind in ("kT", "kip", "vip", "g", "g_rest", "v", "v_rest"):
                    if k == job_at("kT")[0]:
                        for c in range(EC):
                            emptied(pe, c)
                    if kind == "kT":
                        pe.wait_ge(ld_k, 16)
                    elif kind == "kip":
                        pe.wait_ge(ld_kip, 16)
                    elif kind == "vip":
                        pe.wait_ge(ld_vip, 16)
                    elif kind in ("v", "v_rest"):
                        pe.wait_ge(ld_v, 16)
                    if kind in ("kip", "vip"):
                        slot = 0 if kind == "kip" else 1
                        for g in range(CC):
                            for c in range(EC):
                                last = nc.tensor.matmul(
                                    bank[:, g * B * NIP:(g + 1) * B * NIP],
                                    w_stage[:, slot, c, g * P:(g + 1) * P], ctxT[:, c, C_IP:C_IPN],
                                    start=(g == 0 and c == 0), stop=(c == EC - 1), skip_group_check=True)
                        return last
                    for c in range(EC):
                        first, stop = c == 0, c == EC - 1
                        if kind == "kT":
                            last = nc.tensor.matmul(bank[:, 0:C_IP], w_stage[:, 0, c, a * P:(a + 1) * P],
                                                    ctxT[:, c, 0:C_IP], start=first, stop=stop)
                        elif kind == "g":
                            last = nc.tensor.matmul(bank[:, 0:C_ALL], ctxT[:, c, a * P:(a + 1) * P],
                                                    ctxT[:, c, :], start=first, stop=stop)
                        elif kind == "g_rest":
                            last = nc.tensor.matmul(bank[0:B * 32, 0:C_ALL - C_REST],
                                                    ctxT[:, c, C_REST:C_IP], ctxT[:, c, C_REST:C_ALL],
                                                    start=first, stop=stop)
                        elif kind == "v":
                            last = nc.tensor.matmul(bank[:, 0:HALF], ctxT[:, c, a * P:(a + 1) * P],
                                                    w_stage[:, 1, c, h * HALF:(h + 1) * HALF],
                                                    start=first, stop=stop)
                        else:
                            last = nc.tensor.matmul(bank[0:B * 32, 0:HALF], ctxT[:, c, C_REST:C_IP],
                                                    w_stage[:, 1, c, a * HALF:(a + 1) * HALF],
                                                    start=first, stop=stop)
                    return last
                if kind == "mask":
                    pe.wait_ge(ld_small, 32)
                    return nc.tensor.transpose(bank[:, 0:TPB], mask_rows[:], ident[0:TPB, 0:TPB])
                assert kind == "wv"
                pe.wait_ge(ld_out, 16)
                emptied(pe, job_at("vip")[0])
                for c in range(CC):
                    last = nc.tensor.matmul(
                        bank[0:HEADS * NIP, 0:HALF],
                        vip_blk[:, a, c * HEADS * NIP:(c + 1) * HEADS * NIP],
                        wo_sb[:, c, h * HALF:(h + 1) * HALF], start=(c == 0), stop=(c == CC - 1))
                return last

            def transpose_x(s, k):
                pe.wait_ge(ld_x[k % 2], (s * (U // 2) + k // 2 + 1) * 16)
                for c in range(CC):
                    dst = ps[:, BANK_M + c // 4, (c % 4) * P:(c % 4 + 1) * P]
                    last = nc.tensor.transpose(dst, x_in[:, k % 2, c * P:(c + 1) * P], ident[:])
                last.then_inc(xT_psum, 1)

            def queries(s, k):
                for c in range(CC):
                    last = nc.tensor.matmul(ps[:, BANK_M + k % 2, :], wq_sb[:, c, k * P:(k + 1) * P],
                                            xT[:, c, :], start=(c == 0), stop=(c == CC - 1))
                last.then_inc(q_psum, 1)

            def transpose_out(tile):
                pe.wait_ge(text_ready, tile + 1)
                pe.wait_ge(pip_ready, tile + 1)
                for c in range(CC):
                    dst = ps[:, BANK_M + c // 4, (c % 4) * P:(c % 4 + 1) * P]
                    nc.tensor.transpose(dst, text[:, c * HG:(c + 1) * HG, :], ident[:])
                nc.tensor.transpose(ps[0:HEADS * NIP, BANK_M + 1, P:2 * P],
                                    p_ip[:].rearrange("p h n -> p (h n)"), ident[:]).then_inc(oT_psum, 1)

            def output_product(tile, b):
                pe.wait_ge(oT_ready, tile + 1)
                for h in range(2):
                    cols = slice(h * HALF, (h + 1) * HALF)
                    for c in range(CC):
                        nc.tensor.matmul(ps[:, BANK_M + h, 0:HALF], oT[:, c, :], wo_sb[:, c, cols],
                                         start=(c == 0), stop=False)
                    last = nc.tensor.matmul(ps[:, BANK_M + h, 0:HALF], oT[0:HEADS * NIP, 5, :],
                                            wv[:, b, cols], start=False, stop=True)
                last.then_inc(y_psum, 1)

            def main_product(g, b):
                for h2 in range(2):
                    for hh in range(2):
                        j = 2 * h2 + hh
                        nc.tensor.matmul(ps[:, BANK_N + h2, hh * W:(hh + 1) * W], eT[:, j, :],
                                         t_main[:, b, g * HG + j, :], start=(hh == 0), stop=False,
                                         skip_group_check=True)
                    dst = ps[:, BANK_N + h2, 0:2 * W].rearrange("p (h w) -> p h w", h=2)[:, :, 0:WR]
                    last = nc.tensor.matmul(dst, eT_rest[:], t_rest[:, b, g, 2 * h2:2 * h2 + 2, :],
                                            start=False, stop=True, skip_group_check=True)
                last.then_inc(prod, 1)

            pe.wait_ge(ident_ready, 1)
            for k in range(len(jobs)):
                if jobs[k][0] == "kip":
                    pe.wait_ge(ld_q, 16)
                    for t in range(U):
                        if t:
                            pe.wait_ge(xT_ready, t)
                        transpose_x(0, t)
                    pe.wait_ge(xT_ready, U)
                    for t in range(CC):
                        if t >= 2:
                            pe.wait_ge(q_evac, t - 1)
                        queries(0, t)
                run_job(k).then_inc(job_done, 1)
            for k in range(len(jobs) - 4, len(jobs)):
                emptied(pe, k)
            pe.wait_ge(rest_tab, 1)
            pe.wait_ge(zeroed, 4)
            pe.wait_ge(q_evac, CC)

            def bank_free(st, u, g):
                tile = st * U + u
                where = [(uu, gg) for uu in range(U) for gg in range(NG)]
                k = where.index((u, g)) - 1
                while k >= 0 and spare(st, *where[k]) is None:
                    k -= 1
                if k >= 0:
                    kind, n = spare(st, *where[k])
                    t = st * U + where[k][0]
                    if kind == "xT":
                        pe.wait_ge(xT_ready, (st + 1) * U + n + 1)
                    elif kind == "q":
                        pe.wait_ge(q_evac, (st + 1) * CC + n + 1)
                    elif kind == "oT":
                        pe.wait_ge(oT_ready, t)
                    else:
                        pe.wait_ge(y_ready, t)
                elif not is_at(st, 0):
                    pe.wait_ge(y_ready, st * U - 1)

            for st, b in supertiles(pe):
                for u in range(U):
                    tile = st * U + u
                    for g in range(NG):
                        i = st * LG + u * NG + g
                        par = (u * NG + g) % 2
                        first = is_at(st, 0) and u == 0 and g == 0
                        if g == 0:
                            pe.wait_ge(q_ready, tile + 1)
                        for h2 in range(2):
                            last = nc.tensor.matmul(ps[:, BANK_B + h2, 0:2 * TA], q_cur[:, u, g, :],
                                                    k_tab[:, b, 2 * g + h2, :], start=True, stop=True)
                        last.then_inc(scores, 1)
                        if not first:
                            pe.wait_ge(eT_ready, i)
                            if not (is_at(st, 0) and u == 0 and g == 1):
                                pe.wait_ge(dots, i - 1)
                            pb = b
                            if g == 0 and u == 0 and isinstance(st, int) and st % SPB == 0:
                                pb = b - 1
                            main_product((g - 1) % NG, pb)
                        work = spare(st, u, g)
                        if work:
                            bank_free(st, u, g)
                        if work and work[0] == "xT":
                            transpose_x(st + 1, work[1])
                        elif work and work[0] == "q":
                            pe.wait_ge(xT_ready, (st + 2) * U)
                            queries(st + 1, work[1])
                        elif work and work[0] == "oT":
                            transpose_out(tile - 1)
                        elif work and work[0] == "y":
                            pb = b - 1 if u == 0 and isinstance(st, int) and st and st % SPB == 0 else b
                            output_product(tile - 1, pb)
                        pe.wait_ge(e_ready, i + 1)
                        for j in range(HG):
                            nc.tensor.transpose(ps[:, BANK_T, j * P:(j + 1) * P], e[:, par, j, TR:T], ident[:])
                        pe.wait_ge(rest_ready, i + 1)
                        nc.tensor.transpose(ps[:, BANK_T + 1, 0:P], e_rest[:], ident[:]
                                            ).then_inc(eT_psum, 1)
            n = NST * U - 1
            pe.wait_ge(eT_ready, NST * LG)
            pe.wait_ge(dots, NST * LG - 1)
            main_product(NG - 1, B - 1)
            pe.wait_ge(y_ready, n)
            transpose_out(n)
            output_product(n, B - 1)


_INS = ["x", "ctx_2048", "fside_S_0", "L0_xattn_W_q", "L0_xattn_W_k", "L0_xattn_W_v",
        "L0_xattn_W_k_ip", "L0_xattn_W_v_ip", "L0_xattn_W_out", "L0_xattn_b_out"]


def kernel(**inputs):
    import numpy as np
    import concourse.bacc as bacc
    from concourse.bass_utils import run_bass_kernel_spmd

    nc = bacc.Bacc("TRN2", target_bir_lowering=False, num_devices=1)
    arrays, args = {}, []
    for name in _INS:
        a = np.ascontiguousarray(inputs[name])
        arrays[f"in_{name}"] = a
        args.append(nc.dram_tensor(f"in_{name}", a.shape, mybir.dt.from_np(a.dtype),
                                   kind="ExternalInput").ap())
    shape = tuple(inputs["x"].shape)
    out = nc.dram_tensor("out", shape, F32, kind="ExternalOutput").ap()
    xattn_program(nc, *args, out)
    got = run_bass_kernel_spmd(nc, [arrays], core_ids=[0])
    return got.results[0]["out"]
```

```python
from contextlib import ExitStack

import concourse.bass as bass
from concourse import mybir

F32 = mybir.dt.float32
F16 = mybir.dt.float16
ACT = mybir.ActivationFunctionType
ALU = mybir.AluOpType
AX_X = mybir.AxisListType.X

P = 128
HEADS = 20
NIP = 4
EPS = 1e-12
SEM_SCALE = 0.5

BANK_B, BANK_T, BANK_N, BANK_M = 0, 2, 4, 6


def repeated(ap, axis, n):
    shape = list(ap.shape)
    shape[axis] = n
    return ap.broadcast_to(shape)


def xattn_program(nc, x, ctx, mask, w_q, w_k, w_v, w_k_ip, w_v_ip, w_out, b_out, out):
    B, S, C = x.shape
    TA, E = ctx.shape[1:]
    T = TA - NIP
    TR = T - P
    D = C // HEADS
    SCALE = float(D) ** -0.5
    CC = C // P
    EC = E // P
    HG = P // D
    NG = HEADS // HG
    NPR = HEADS // 2
    TPB = S // P
    NT = B * TPB
    HALF = C // 2
    NHN = HEADS * NIP
    W = D + NIP + 1 + T
    W_A, W_Z, W_G = D, D + NIP, D + NIP + 1
    WR = W_G + TR
    HI, LO = 0, 1
    assert D == 32 and NG == CC == 5 and 0 < TR <= D and TA * 2 <= 512 and W * 2 <= 512

    C_REST = B * P
    C_IP = C_REST + B * 32
    C_IPN = C_IP + B * NIP
    C_ALL = C_IPN + B * NIP

    x_t = x.rearrange("b (t p) c -> (b t) p c", p=P)
    out_t = out.rearrange("b (t p) c -> (b t) p c", p=P)

    with ExitStack() as stack:
        def sb(name, shape, dt=F32):
            return stack.enter_context(nc.sbuf_tensor(name, shape, dt))

        def sem(name):
            return stack.enter_context(nc.semaphore(name))

        ps = stack.enter_context(nc.psum_tensor("ps", [P, 8, 512], F32))
        ps_m = ps[:, BANK_M:BANK_M + 2, :].rearrange("p b n -> p (b n)")

        ident = sb("ident", [P, P])
        ident16 = sb("ident16", [P, P], F16)
        minus_half = sb("minus_half", [P, HEADS])
        tiny = sb("tiny", [P, 1])
        p_up = sb("p_up", [P, 1])
        wq_hl = sb("wq_hl", [P, 2, CC, C], F16)
        wo_hl = sb("wo_hl", [P, 2, CC, C], F16)
        wv_hl = sb("wv_hl", [P, 2, B, C], F16)
        mask_sb = sb("mask_sb", [P, TPB])
        bias_sb = sb("bias_sb", [P, C])
        k_tab = sb("k_tab", [P, B, HG, NG, TA], F16)
        t_main = sb("t_main", [P, 2, B, HEADS, W], F16)
        t_rest = sb("t_rest", [P, 2, B, NPR, 2, WR], F16)
        x_in = sb("x_in", [P, 2, C])
        fac = sb("fac", [P, 32])
        mx = sb("mx", [P, 16])

        AREA = 29200
        area = sb("area", [P, AREA])
        cut = [0]

        def part(rows, *dims, dt=F32):
            n = 1
            for d in dims:
                n *= d
            words = n if dt == F32 else (n + 1) // 2
            view = area[0:rows, cut[0]:cut[0] + words]
            cut[0] += words
            assert cut[0] <= AREA
            if dt != F32:
                view = view.bitcast(dt)
            if len(dims) == 1:
                return view
            names = "abcd"[:len(dims)]
            return view.rearrange(f"p ({' '.join(names)}) -> p {' '.join(names)}",
                                  **dict(zip(names[1:], dims[1:])))

        ctx_main = part(P, B, E)
        ctx_rest = part(B * 32, E)
        ip_raw = part(B * NIP, E)
        ip_nrm = part(B * NIP, E)
        ip_sq = part(B * NIP, 1)
        ip_sqg = part(B * NIP, 1)
        ip_rn = part(B * NIP, 1)
        ctxT = part(P, EC, C_ALL)
        mask_rows = part(TPB, P)
        vip_blk = part(P, B, CC * (NHN // CC + NHN))
        w_stage = part(P, 2, EC, C)
        wq_sb = part(P, CC, C)
        wo_sb = part(P, CC, C)
        k_nat = part(P, 2, B, NG, TA, dt=F16)
        g_nat = part(P, 2, B, W - D + 1, dt=F16)
        v_rest = part(B * 32, 2, C, dt=F16)
        g_rest = part(B * 32, 2, WR - D + 1, dt=F16)

        cut[0] = 0
        e = part(P, NG, HG, T)
        e_rest = part(P, 2, 2, 2, 32, dt=F16)
        rest_up = part(P, 2, 2, 32)
        eT = part(P, 2, 2, HG * P, dt=F16)
        rT = part(P, 2, 2, P, dt=F16)
        stats = part(P, 2, HEADS, W_G)
        text = part(P, HEADS, D)
        oT = part(P, 2, CC + 1, P, dt=F16)
        x_res = part(P, 2, C)
        y = part(P, 2, C)
        x_hat = part(P, C)
        x_junk = part(P, C)
        xT = part(P, 2, CC, P, dt=F16)
        q_hl = part(P, 2, CC * P, dt=F16)
        q_stack = part(P, 2, HG, NG * P, dt=F16)
        x_sq = part(P, 2)
        x_sqg = part(P, 2)
        x_rn = part(P, 2)
        row_n = part(P, 2)
        row_c = part(P, 2)
        row_ip = part(P, 2)
        s_max = part(P, 2, HG)
        s_bias = part(P, 2, HG)
        ege = part(P, 2, HEADS)
        ip_score = part(P, 2, HEADS, NIP)
        ip_kept = part(P, HEADS, NIP)
        z_inv = part(P, HEADS)
        z_rho = part(P, HEADS)
        z_sq = part(P, HEADS)
        n_sq = part(P, HEADS)
        n_inv = part(P, HEADS)
        sem_raw = part(P, HEADS, NIP)
        fused = part(P, HEADS, NIP)
        f_max = part(P, HEADS)
        f_diff = part(P, HEADS, NIP)
        e_ip = part(P, HEADS, NIP)
        ip_sum = part(P, HEADS)
        ip_inv = part(P, HEADS)
        ip_w = part(P, HEADS)
        p_ip = part(P, P)

        (R_CTX, R_WK, R_WKI, R_WV, R_WVI, R_WQ, R_WO, KF, KIF, VF, AF, GF, G2F, WQF, WOF, C1, C2,
         RHO, WVF, YM, GSC, R_WVJ, SCR0, SCR1, SCR2, N_WVJ) = range(26)
        (N_CTX, N_WK, N_WKI, N_WV, N_WVI, N_WQ, N_WO, M0) = range(8)

        def F(k):
            return fac[:, k:k + 1]

        def N(k):
            return mx[:, k:k + 1]

        ld_ctx, ld_ip, ld_k, ld_v, ld_kip, ld_vip, ld_q, ld_out, ld_small = (
            sem(f"ld_{n}") for n in ("ctx", "ip", "k", "v", "kip", "vip", "q", "out", "small"))
        ident_ready, zeroed, half_ready, ident_zero, ip_sq_ready, ip_guard, ip_rn_ready, ip_nrm_ready = (
            sem(n) for n in ("ident_ready", "zeroed", "half_ready", "ident_zero", "ip_sq_ready",
                             "ip_guard", "ip_rn_ready", "ip_nrm_ready"))
        part_max, all_max, fac_link, fac_ready = (
            sem(n) for n in ("part_max", "all_max", "fac_link", "fac_ready"))
        job_done, job_act, job_dve = sem("job_done"), sem("job_act"), sem("job_dve")
        wsplit_hi, wsplit_lo, k_stacked, tables_ready = (
            sem(n) for n in ("wsplit_hi", "wsplit_lo", "k_stacked", "tables_ready"))
        ld_x = [sem("ld_x0"), sem("ld_x1")]
        ld_qs = [sem("ld_qs0"), sem("ld_qs1")]
        ld_res = [sem("ld_res0"), sem("ld_res1")]
        st_y = [sem("st_y0"), sem("st_y1")]
        xsq_ready, xsq_guard, xrn_ready, xhat_ready, rown_ready, rowc_ready = (
            sem(n) for n in ("xsq_ready", "xsq_guard", "xrn_ready", "xhat_ready", "rown_ready", "rowc_ready"))
        xT_psum, xT_hi, xT_lo, q_psum, q_hi, q_lo = (
            sem(n) for n in ("xT_psum", "xT_hi", "xT_lo", "q_psum", "q_hi", "q_lo"))
        scores, max_ready, bias_ready, e_ready, rest_scaled, rest_hi, rest_lo = (
            sem(n) for n in ("scores", "max_ready", "bias_ready", "e_ready", "rest_scaled", "rest_hi",
                             "rest_lo"))
        eT_psum, rT_psum, eT_hi, eT_lo, rT_ready, prod, stats_ready, dots = (
            sem(n) for n in ("eT_psum", "rT_psum", "eT_hi", "eT_lo", "rT_ready", "prod", "stats_ready", "dots"))
        z_link, z_ready, text_ready, nsq_ready, ninv_ready, chain = (
            sem(n) for n in ("z_link", "z_ready", "text_ready", "nsq_ready", "ninv_ready", "chain"))
        ip_kept_ready, ip_ready = sem("ip_kept_ready"), sem("ip_ready")
        diff_ready, eip_ready, ipw_ready, pip_ready, pip_zero = (
            sem(n) for n in ("diff_ready", "eip_ready", "ipw_ready", "pip_ready", "pip_zero"))
        oT_psum, oT_hi, oT_lo, y_psum, y_ready, res_ready = (
            sem(n) for n in ("oT_psum", "oT_hi", "oT_lo", "y_psum", "y_ready", "res_ready"))

        block = stack.enter_context(nc.Block())

        jobs = [("ctxT", c, 0, "act" if c % 2 else "dve") for c in range(EC)]
        jobs += [("kT", g, 0, "both") for g in range(NG)]
        jobs += [("v", b, h, "both") for b in range(B) for h in range(2)]
        jobs += [("v_rest", h, 0, "both") for h in range(2)]
        jobs += [("kip", 0, 0, "both")]
        jobs += [("g", b, 0, "both") for b in range(B)] + [("g_rest", 0, 0, "both")]
        jobs += [("mask", 0, 0, "act"), ("vip", 0, 0, "act")]
        jobs += [("wv", b, h, "both") for b in range(B) for h in range(2)]

        def job_at(kind):
            return [k for k, j in enumerate(jobs) if j[0] == kind]

        def by_act(k):
            return sum(j[3] in ("act", "both") for j in jobs[:k + 1])

        def by_dve(k):
            return sum(j[3] in ("dve", "both") for j in jobs[:k + 1])

        def emptied(eng, k):
            if jobs[k][3] == "act":
                eng.wait_ge(job_act, by_act(k))
            else:
                eng.wait_ge(job_dve, by_dve(k))

        def prepared(eng):
            eng.wait_ge(job_done, len(jobs))
            eng.wait_ge(job_act, by_act(len(jobs) - 1))
            eng.wait_ge(job_dve, by_dve(len(jobs) - 1))
            eng.wait_ge(wsplit_lo, 2)
            eng.wait_ge(tables_ready, 1)
            eng.wait_ge(k_stacked, 16 * 4 * HG)

        NP, PPB = NT // 2, TPB // 2
        SEGMENTS = []
        for b in range(B):
            lo, hi = b * PPB, (b + 1) * PPB
            SEGMENTS += [(lo, lo + 1, b), (lo + 1, hi - 1, b), (hi - 1, hi, b)]

        def tiles(eng):
            for lo, hi, b in SEGMENTS:
                if hi - lo == 1:
                    for u in range(2):
                        yield lo * 2 + u, u, b, lo == b * PPB
                else:
                    with eng.Fori(lo, hi) as pair:
                        for u in range(2):
                            yield pair * 2 + u, u, b, False

        def known(n):
            return isinstance(n, int)

        def before(n, k):
            return known(n) and n < k

        def loads_ahead(n):
            return not known(n) or n + 2 < NT

        @block.sync
        def _(sp):
            for b in range(B):
                sp.dma_start(ctx_main[:, b, :], ctx[b, TR:T, :]).then_inc(ld_ctx, 16)
                sp.dma_start(ctx_rest[b * 32:b * 32 + 32, :], ctx[b, 0:32, :]).then_inc(ld_ctx, 16)
                sp.dma_start(ip_raw[b * NIP:(b + 1) * NIP, :], ctx[b, T:TA, :]).then_inc(ld_ip, 16)
            sp.dma_start(w_stage[:, 0], w_k.rearrange("(c p) n -> p c n", p=P)).then_inc(ld_k, 16)
            sp.dma_start(w_stage[:, 1], w_v.rearrange("(c p) n -> p c n", p=P)).then_inc(ld_v, 16)
            sp.dma_start(wq_sb, w_q.rearrange("(c p) n -> p c n", p=P)).then_inc(ld_q, 16)
            sp.dma_start(wo_sb, w_out.rearrange("(c p) n -> p c n", p=P)).then_inc(ld_out, 16)
            sp.dma_start(mask_rows, mask.rearrange("(t p) -> t p", p=P)).then_inc(ld_small, 16)
            sp.dma_start(bias_sb[:], repeated(b_out.rearrange("(a n) -> a n", a=1), 0, P)
                         ).then_inc(ld_small, 16)

            def load_x(n, u):
                sp.dma_start(x_in[:, u, :], x_t[n]).then_inc(ld_x[u], 16)

            load_x(0, 0)
            load_x(1, 1)
            sp.wait_ge(job_done, job_at("kT")[-1] + 1)
            sp.wait_ge(part_max, 2)
            sp.dma_start(w_stage[:, 0], w_k_ip.rearrange("(c p) n -> p c n", p=P)).then_inc(ld_kip, 16)
            sp.wait_ge(job_done, job_at("v_rest")[-1] + 1)
            sp.wait_ge(part_max, 3)
            sp.dma_start(w_stage[:, 1], w_v_ip.rearrange("(c p) n -> p c n", p=P)).then_inc(ld_vip, 16)
            sp.wait_ge(job_dve, by_dve(job_at("kip")[0]))
            for hl in range(2):
                for j in range(HG):
                    for k in (hl, 2 + hl):
                        sp.dma_start(k_tab[32 * k:32 * k + 32, :, j, :, :],
                                     k_nat[32 * j:32 * j + 32, hl]).then_inc(k_stacked, 16)

            def stack_queries(n, u):
                if not before(n, 2):
                    sp.wait_ge(scores, (n - 1) * NG)
                sp.wait_ge(q_hi, n + 1)
                sp.wait_ge(q_lo, n + 1)
                for hl in range(2):
                    for j in range(HG):
                        for k in (2 * hl, 2 * hl + 1):
                            sp.dma_start(q_stack[32 * k:32 * k + 32, u, j, :],
                                         q_hl[32 * j:32 * j + 32, hl, :]).then_inc(ld_qs[u], 16)

            prepared(sp)
            stack_queries(0, 0)
            stack_queries(1, 1)
            for n, u, _b, _f in tiles(sp):
                if loads_ahead(n):
                    sp.wait_ge(xhat_ready, n + 1)
                    load_x(n + 2, u)
                if not before(n, 1):
                    if not before(n, 3):
                        sp.wait_ge(y_ready, n - 2)
                    sp.dma_start(x_res[:, 1 - u, :], x_t[n - 1]).then_inc(ld_res[1 - u], 16)
                    if not (known(n) and n + 1 >= NT):
                        stack_queries(n + 1, 1 - u)
                if not before(n, 2):
                    sp.wait_ge(y_ready, n - 1)
                    sp.dma_start(out_t[n - 2], y[:, u, :]).then_inc(st_y[u], 16)
            sp.wait_ge(y_ready, NT - 2)
            sp.dma_start(x_res[:, 1, :], x_t[NT - 1]).then_inc(ld_res[1], 16)
            for n in (NT - 2, NT - 1):
                sp.wait_ge(y_ready, n + 1)
                sp.dma_start(out_t[n], y[:, n % 2, :]).then_inc(st_y[n % 2], 16)
            for k in range(2):
                sp.wait_ge(st_y[k], 16 * NT // 2)

        @block.gpsimd
        def _(pool):
            nc.gpsimd.memset(ident[:], 0.0).then_inc(ident_zero, 1)
            pool.wait_ge(ident_zero, 1)
            nc.gpsimd.affine_select(out=ident[:], in_=ident[:], compare_op=ALU.not_equal, fill=1.0,
                                    base=0, pattern=[[-1, P]], channel_multiplier=1
                                    ).then_inc(ident_ready, 1)
            nc.gpsimd.memset(minus_half[:], -0.5).then_inc(half_ready, 1)
            nc.gpsimd.memset(tiny[:], 1e-36).then_inc(half_ready, 1)
            nc.gpsimd.memset(p_up[:], 2.0 ** 14).then_inc(half_ready, 1)
            pool.wait_ge(ident_ready, 1)
            nc.gpsimd.tensor_copy(ident16[:], ident[:]).then_inc(ident_ready, 1)
            pool.wait_ge(ip_guard, 1)
            pool.wait_ge(half_ready, 3)
            nc.gpsimd.tensor_tensor(ip_rn, ip_sqg, minus_half[0:B * NIP, 0:1], ALU.pow
                                    ).then_inc(ip_rn_ready, 1)

            def across(k, m):
                pool.wait_ge(part_max, k + 1)
                nc.gpsimd.partition_all_reduce(N(m), N(M0 + m), P, bass.bass_isa.ReduceOp.max
                                               ).then_inc(all_max, 1)

            across(0, N_CTX)
            across(1, N_WK)
            nc.gpsimd.memset(t_rest[:], 0.0).then_inc(zeroed, 1)
            across(2, N_WV)
            nc.gpsimd.memset(vip_blk, 0.0).then_inc(zeroed, 1)
            for hl in range(2):
                one = 1.0 if hl == HI else 0.0
                nc.gpsimd.memset(g_nat[:, hl, :, NIP:NIP + 1], one).then_inc(zeroed, 1)
                nc.gpsimd.memset(g_rest[:, hl, NIP:NIP + 1], one).then_inc(zeroed, 1)
            across(3, N_WQ)
            across(4, N_WO)
            across(5, N_WKI)
            across(6, N_WVI)
            prepared(pool)
            nc.gpsimd.memset(p_ip, 0.0).then_inc(pip_zero, 1)

            def unit_rows(n, u):
                pool.wait_ge(xsq_ready, n + 1)
                nc.gpsimd.tensor_tensor(x_sqg[:, u:u + 1], x_sq[:, u:u + 1], tiny[:], ALU.add
                                        ).then_inc(xsq_guard, 1)
                pool.wait_ge(xsq_guard, n + 1)
                if not before(n, 2):
                    pool.wait_ge(rown_ready, n - 1)
                nc.gpsimd.tensor_tensor(x_rn[:, u:u + 1], x_sqg[:, u:u + 1], minus_half[:, 0:1], ALU.pow
                                        ).then_inc(xrn_ready, 1)
                pool.wait_ge(xrn_ready, n + 1)
                if not before(n, 1):
                    pool.wait_ge(xT_psum, n)
                nc.gpsimd.tensor_tensor(x_hat, x_in[:, u, :], repeated(x_rn[:, u:u + 1], 1, C), ALU.mult
                                        ).then_inc(xhat_ready, 1)

            def norm_inverse(n, half):
                heads = slice(half * HEADS // 2, (half + 1) * HEADS // 2)
                pool.wait_ge(nsq_ready, n + 1)
                nc.gpsimd.tensor_tensor(n_inv[:, heads], n_sq[:, heads], minus_half[:, heads], ALU.pow
                                        ).then_inc(ninv_ready, 1)

            def text_part(n, u):
                pool.wait_ge(z_ready, n + 1)
                if not before(n, 1):
                    pool.wait_ge(oT_psum, n)
                nc.gpsimd.tensor_tensor(text, stats[:, u, :, 0:D],
                                        repeated(z_rho.rearrange("p (h a) -> p h a", a=1), 2, D), ALU.mult
                                        ).then_inc(text_ready, 1)

            def residual(n, u):
                pool.wait_ge(ld_res[u], (n - u + 2) * 8)
                nc.gpsimd.tensor_tensor(x_res[:, u, :], x_res[:, u, :], bias_sb[:], ALU.add
                                        ).then_inc(res_ready, 1)

            def split_rest(i, g):
                src = e[:, g, :, 0:32].rearrange("p (a h) t -> p a h t", a=2)
                up = repeated(repeated(repeated(p_up[:].rearrange("p (a h t) -> p a h t", a=1, h=1), 3, 32), 2, 2),
                              1, 2)
                pool.wait_ge(e_ready, i + 1)
                if not (known(i) and i < 1):
                    pool.wait_ge(rT_psum, i)
                nc.gpsimd.tensor_tensor(rest_up, src, up, ALU.mult).then_inc(rest_scaled, 1)
                nc.gpsimd.tensor_tensor(e_rest[:, :, HI], src, up, ALU.mult).then_inc(rest_hi, 1)
                pool.wait_ge(rest_scaled, i + 1)
                pool.wait_ge(rest_hi, i + 1)
                nc.gpsimd.tensor_tensor(e_rest[:, :, LO], rest_up, e_rest[:, :, HI], ALU.subtract
                                        ).then_inc(rest_lo, 1)

            unit_rows(0, 0)
            unit_rows(1, 1)
            for n, u, _b, _f in tiles(pool):
                for g in range(NG):
                    split_rest(n * NG + g, g)
                    if g == 1 and not before(n, 2):
                        residual(n - 2, u)
                    if g == 2 and loads_ahead(n):
                        unit_rows(n + 2, u)
                    if g == 2 and not before(n, 1):
                        text_part(n - 1, 1 - u)
                    if g in (3, 4) and not before(n, 1):
                        norm_inverse(n - 1, g - 3)
            residual(NT - 2, 0)
            norm_inverse(NT - 1, 0)
            norm_inverse(NT - 1, 1)
            text_part(NT - 1, 1)
            residual(NT - 1, 1)

        def empty(k, high, low, plain):
            kind, a, h, _ = jobs[k]
            bank = ps[:, k % 4, :]

            def both(dst, src, k, rows=slice(0, P)):
                f = fac[rows, k:k + 1]
                if high:
                    return high(dst(HI), src, f)
                return low(dst(LO), src, f, dst(HI))

            if kind == "ctxT":
                return plain(ctxT[:, a, :], bank[:, 0:C_ALL])
            if kind == "mask":
                return plain(mask_sb[:], bank[:, 0:TPB])
            if kind == "kT":
                for b in range(B):
                    both(lambda hl: k_nat[:, hl, b, a, 0:TR],
                         bank[:, C_REST + 32 * b:C_REST + 32 * b + TR], KF)
                    last = both(lambda hl: k_nat[:, hl, b, a, TR:T], bank[:, P * b:P * b + P], KF)
                return last
            if kind == "kip":
                src = bank[:, 0:CC * B * NIP].rearrange("p (g n) -> p g n", g=CC)
                for b in range(B):
                    last = both(lambda hl: k_nat[:, hl, b, :, T:TA], src[:, :, b * NIP:(b + 1) * NIP], KIF)
                return last
            if kind == "g":
                both(lambda hl: g_nat[:, hl, a, 0:NIP], bank[:, C_IPN + NIP * a:C_IPN + NIP * a + NIP], AF)
                both(lambda hl: g_nat[:, hl, a, NIP + 1:NIP + 1 + TR],
                     bank[:, C_REST + 32 * a:C_REST + 32 * a + TR], G2F)
                return both(lambda hl: g_nat[:, hl, a, NIP + 1 + TR:NIP + 1 + T], bank[:, P * a:P * a + P], GF)
            if kind == "g_rest":
                for b in range(B):
                    r = slice(32 * b, 32 * b + 32)
                    lo = C_IPN - C_REST + NIP * b
                    both(lambda hl: g_rest[r, hl, 0:NIP], bank[r, lo:lo + NIP], AF, r)
                    last = both(lambda hl: g_rest[r, hl, NIP + 1:NIP + 1 + TR],
                                bank[r, 32 * b:32 * b + TR], GF, r)
                return last
            if kind == "v":
                return both(lambda hl: t_main[:, hl, a, h * 10:h * 10 + 10, 0:D],
                            bank[:, 0:HALF].rearrange("p (n d) -> p n d", d=D), VF)
            if kind == "v_rest":
                return both(lambda hl: v_rest[:, hl, a * HALF:(a + 1) * HALF], bank[0:B * 32, 0:HALF], VF,
                            slice(0, B * 32))
            if kind == "vip":
                step = NHN + HG * NIP
                for b in range(B):
                    for j in range(HG):
                        q = slice(D * j, D * j + D)
                        dst = vip_blk[q, b, :].rearrange("p (g r) -> p g r", r=step)
                        src = bank[q, 0:CC * B * NIP].rearrange("p (g n) -> p g n", g=CC)
                        last = plain(dst[:, :, j * NIP:(j + 1) * NIP], src[:, :, b * NIP:(b + 1) * NIP])
                return last
            assert kind == "wv"
            return both(lambda hl: wv_hl[:, hl, a, h * HALF:(h + 1) * HALF], bank[:, 0:HALF], WVF)

        FACTORS = {"kT": 1, "v": 2, "v_rest": 2, "kip": 5, "g": 1, "g_rest": 1, "wv": 6}
        X_UP, Q_DOWN, P_UP = 2.0 ** 10, 2.0 ** -8, 2.0 ** 14

        @block.scalar
        def _(act):
            def copy(o, i, scale=1.0):
                return nc.scalar.activation(o, i, ACT.Copy, scale=scale)

            def split_weight(done, loaded, dst, src, factors, f):
                act.wait_ge(loaded, 16)
                act.wait_ge(fac_ready, factors)
                copy(dst, src, F(f)).then_inc(wsplit_hi, 1)

            for k in range(len(jobs)):
                kind, who = jobs[k][0], jobs[k][3]
                if k == job_at("kip")[0]:
                    split_weight(0, ld_q, wq_hl[:, HI], wq_sb, 3, WQF)
                    split_weight(1, ld_out, wo_hl[:, HI], wo_sb, 4, WOF)
                if who == "dve":
                    continue
                act.wait_ge(job_done, k + 1)
                if kind in FACTORS:
                    act.wait_ge(fac_ready, FACTORS[kind])
                if kind == "vip":
                    act.wait_ge(zeroed, 2)
                empty(k, copy, None, copy).then_inc(job_act, 1)
            prepared(act)

            def row_squares(n, u):
                act.wait_ge(ld_x[u], (n - u + 2) * 8)
                if not before(n, 1):
                    act.wait_ge(xsq_guard, n)
                nc.scalar.activation(x_junk, x_in[:, u, :], ACT.Square, accum_out=x_sq[:, u:u + 1]
                                     ).then_inc(xsq_ready, 1)

            def x_high(n):
                act.wait_ge(xT_psum, n + 1)
                if not before(n, 1):
                    act.wait_ge(q_psum, n)
                copy(xT[:, HI], ps_m[:, 0:C].rearrange("p (c s) -> p c s", c=CC), X_UP
                     ).then_inc(xT_hi, 1)

            def q_high(n, u):
                act.wait_ge(q_psum, n + 1)
                if not before(n, 1):
                    act.wait_ge(ld_qs[1 - u], (n + u) * 128)
                copy(q_hl[:, HI, :], ps_m[:, 0:C], Q_DOWN).then_inc(q_hi, 1)

            def e_high(i, par):
                act.wait_ge(eT_psum, i + 1)
                if not (known(i) and i < 2):
                    act.wait_ge(prod, i - 1)
                copy(eT[:, par, HI, :], ps[:, BANK_T, :], P_UP).then_inc(eT_hi, 1)

            def copy_rest(i, par):
                act.wait_ge(rT_psum, i + 1)
                copy(rT[:, par].rearrange("p a s -> p (a s)"),
                     ps[:, BANK_T + 1, 0:P].bitcast(F16)).then_inc(rT_ready, 1)

            def copy_stats(i, g, u):
                act.wait_ge(dots, i + 1)
                src = ps[:, BANK_N:BANK_N + 2, 0:2 * W].rearrange("p b (h w) -> p b h w", h=2)
                dst = stats[:, u, g * HG:(g + 1) * HG, :].rearrange("p (b h) w -> p b h w", b=2)
                copy(dst, src[:, :, :, 0:W_G]).then_inc(stats_ready, 1)

            def exps(i, par, g, u):
                act.wait_ge(max_ready, i + 1)
                src = ps[:, BANK_B:BANK_B + 2, 0:2 * TA].rearrange("p b (h t) -> p b h t", h=2)
                copy(ip_score[:, u, g * HG:(g + 1) * HG, :].rearrange("p (b h) n -> p b h n", b=2),
                     src[:, :, :, T:TA], row_ip[:, u:u + 1]).then_inc(ip_ready, 1)
                act.wait_ge(bias_ready, i + 1)
                if not (known(i) and i < NG):
                    act.wait_ge(dots, i - NG + 1)
                for j in range(HG):
                    src = ps[:, BANK_B + j // 2, (j % 2) * TA:(j % 2) * TA + T]
                    last = nc.scalar.activation(e[:, g, j, :], src, ACT.Exp, bias=s_bias[:, par, j:j + 1],
                                                scale=row_c[:, u:u + 1])
                last.then_inc(e_ready, 1)

            def exp_ip(n):
                act.wait_ge(diff_ready, n + 1)
                nc.scalar.activation(e_ip, f_diff, ACT.Exp).then_inc(eip_ready, 1)

            def out_high(n):
                act.wait_ge(oT_psum, n + 1)
                if not before(n, 1):
                    act.wait_ge(y_psum, 2 * n)
                copy(oT[:, HI], ps_m[:, 0:C + P].rearrange("p (c s) -> p c s", c=CC + 1)
                     ).then_inc(oT_hi, 1)

            for n in range(2):
                row_squares(n, n)
            for n in range(2):
                x_high(n)
                q_high(n, n)
            exps(0, 0, 0, 0)
            for n, u, _b, _f in tiles(act):
                for g in range(NG):
                    i = n * NG + g
                    par = (u * NG + g) % 2
                    if g == 0 and not before(n, 1) and not (known(n) and n + 1 >= NT):
                        q_high(n + 1, 1 - u)
                    if g == 1 and not before(n, 2):
                        out_high(n - 2)
                    if g == 4 and loads_ahead(n):
                        x_high(n + 2)
                    e_high(i, par)
                    if not (known(i) and i == NT * NG - 1):
                        exps(i + 1, 1 - par, (g + 1) % NG, u if g < NG - 1 else 1 - u)
                    copy_rest(i, par)
                    if not (known(i) and i < 1):
                        copy_stats(i - 1, (g - 1) % NG, u if g >= 1 else 1 - u)
                    if g == 1 and loads_ahead(n):
                        row_squares(n + 2, u)
                    if g == 4 and not before(n, 1):
                        exp_ip(n - 1)
            copy_stats(NT * NG - 1, NG - 1, 1)
            out_high(NT - 2)
            exp_ip(NT - 1)
            out_high(NT - 1)

        @block.vector
        def _(dve):
            def ts(o, i, s1, s2=None, op0=ALU.mult, op1=None):
                if s2 is None:
                    return nc.vector.tensor_scalar(o, i, s1, None, op0)
                return nc.vector.tensor_scalar(o, i, s1, s2, op0, op1 or ALU.mult)

            def low_part(o, i, f, high):
                return nc.vector.scalar_tensor_tensor(out=o, in0=i, scalar=f, in1=high, op0=ALU.mult,
                                                      op1=ALU.subtract)

            links = [0]

            def link(ins):
                links[0] += 1
                ins.then_inc(fac_link, 1)
                dve.wait_ge(fac_link, links[0])

            def largest(dst, src):
                return nc.vector.tensor_reduce(dst, src, axis=AX_X, op=ALU.max, apply_absolute_value=True)

            def magnitude(m, k, src, r):
                if src is not None:
                    flat = src.rearrange("p a n -> p (a n)")
                    largest(N(M0 + m), flat).then_inc(part_max, 1)
                dve.wait_ge(all_max, k + 1)
                link(ts(N(m), N(m), 1e-15, op0=ALU.max))
                link(nc.vector.reciprocal(F(r), N(m)))

            dve.wait_ge(ld_ip, 16 * B)
            nc.vector.tensor_tensor_reduce(out=ip_nrm, in0=ip_raw, in1=ip_raw, scale=1.0,
                                           scalar=0.0, op0=ALU.mult, op1=ALU.add,
                                           accum_out=ip_sq).then_inc(ip_sq_ready, 1)
            dve.wait_ge(ip_sq_ready, 1)
            ts(ip_sqg, ip_sq, EPS * EPS, op0=ALU.max).then_inc(ip_guard, 1)
            link(nc.vector.memset(fac[:, SCR0:SCR2 + 1], 0.0))
            dve.wait_ge(ld_ctx, 32 * B)
            link(largest(fac[0:P, SCR0:SCR0 + 1], ctx_main.rearrange("p a n -> p (a n)")))
            link(largest(fac[0:B * 32, SCR1:SCR1 + 1], ctx_rest))
            link(largest(fac[0:B * NIP, SCR2:SCR2 + 1], ip_raw))
            largest(N(M0 + N_CTX), fac[:, SCR0:SCR2 + 1]).then_inc(part_max, 1)
            dve.wait_ge(ip_rn_ready, 1)
            ts(ip_nrm, ip_raw, ip_rn).then_inc(ip_nrm_ready, 1)

            def factors(kind):
                if kind == "kT":
                    magnitude(N_CTX, 0, None, R_CTX)
                    link(ts(F(AF), F(R_CTX), 2.0 ** 9))
                    link(ts(F(GF), F(R_CTX), F(R_CTX)))
                    link(ts(F(GSC), F(GF), EPS * EPS * 2.0 ** -10))
                    link(ts(F(GSC), F(GSC), 1e-37, op0=ALU.max))
                    link(ts(F(G2F), F(GF), 2.0 ** 5))
                    link(ts(F(GF), F(GF), 2.0 ** 4))
                    dve.wait_ge(ld_k, 16)
                    magnitude(N_WK, 1, w_stage[:, 0], R_WK)
                    link(ts(F(KF), F(R_WK), F(R_CTX)))
                    ts(F(KF), F(KF), SCALE * 2.0 ** 4).then_inc(fac_ready, 1)
                elif kind == "v":
                    dve.wait_ge(ld_v, 16)
                    magnitude(N_WV, 2, w_stage[:, 1], R_WV)
                    link(ts(F(VF), F(R_WV), F(R_CTX)))
                    ts(F(VF), F(VF), 2.0 ** 4).then_inc(fac_ready, 1)
                elif kind == "kip":
                    dve.wait_ge(ld_q, 16)
                    magnitude(N_WQ, 3, wq_sb, R_WQ)
                    ts(F(WQF), F(R_WQ), 2.0 ** 8).then_inc(fac_ready, 1)
                    dve.wait_ge(ld_out, 16)
                    magnitude(N_WO, 4, wo_sb, R_WO)
                    ts(F(WOF), F(R_WO), 2.0 ** 8).then_inc(fac_ready, 1)
                    dve.wait_ge(ld_kip, 16)
                    magnitude(N_WKI, 5, w_stage[:, 0], R_WKI)
                    link(ts(F(KIF), F(R_WKI), F(R_CTX)))
                    link(ts(F(KIF), F(KIF), SCALE * 2.0 ** 4))
                    link(ts(F(SCR0), N(N_WQ), N(N_CTX)))
                    link(ts(F(SCR0), F(SCR0), 2.0 ** -14))
                    link(ts(F(C1), F(SCR0), N(N_WK)))
                    ts(F(C2), F(SCR0), N(N_WKI)).then_inc(fac_ready, 1)
                    dve.wait_ge(wsplit_hi, 1)
                    dve.wait_ge(fac_ready, 4)
                    low_part(wq_hl[:, LO], wq_sb, F(WQF), wq_hl[:, HI]).then_inc(wsplit_lo, 1)
                    dve.wait_ge(wsplit_hi, 2)
                    low_part(wo_hl[:, LO], wo_sb, F(WOF), wo_hl[:, HI]).then_inc(wsplit_lo, 1)
                elif kind == "wv":
                    dve.wait_ge(ld_vip, 16)
                    magnitude(N_WVI, 6, w_stage[:, 1], R_WVI)
                    link(nc.vector.tensor_tensor(F(N_WVJ), N(N_WVI), N(N_WV), ALU.max))
                    link(nc.vector.reciprocal(F(R_WVJ), F(N_WVJ)))
                    link(ts(F(RHO), N(N_WV), F(R_WVJ)))
                    link(ts(F(SCR0), F(R_WVJ), F(R_CTX)))
                    link(ts(F(SCR0), F(SCR0), 2.0 ** -2))
                    link(ts(F(SCR1), F(N_WVJ), N(N_CTX)))
                    link(ts(F(SCR1), F(SCR1), 2.0 ** -12))
                    link(ts(F(YM), F(SCR1), N(N_WO)))
                    ts(F(WVF), F(SCR0), F(R_WO)).then_inc(fac_ready, 1)

            for k in range(len(jobs)):
                kind, who = jobs[k][0], jobs[k][3]
                if k == job_at(kind)[0]:
                    factors(kind)
                if kind == "mask":
                    dve.wait_ge(job_dve, by_dve(k))
                    dve.wait_ge(zeroed, 6)
                    for hl in range(2):
                        for b in range(B):
                            src = g_nat[:, hl, b:b + 1, 0:W - D]
                            nc.vector.tensor_copy(t_main[:, hl, b, :, D:W], repeated(src, 1, HEADS))
                            for q in range(4):
                                rows, r = slice(32 * q, 32 * q + TR), slice(32 * b, 32 * b + TR)
                                vr = v_rest[r, hl, :].rearrange("p (n h d) -> p n h d", h=2, d=D)
                                nc.vector.tensor_copy(t_rest[rows, hl, b, :, q % 2, 0:D], vr[:, :, q % 2, :])
                                last = nc.vector.tensor_copy(
                                    t_rest[rows, hl, b, :, q % 2, D:WR],
                                    repeated(g_rest[r, hl:hl + 1, 0:WR - D], 1, NPR))
                    last.then_inc(tables_ready, 1)
                if who == "act":
                    continue
                dve.wait_ge(job_done, k + 1)
                if who == "both":
                    dve.wait_ge(job_act, by_act(k))
                    dve.wait_ge(fac_ready, FACTORS[kind])
                empty(k, None, low_part, nc.vector.tensor_copy
                      ).then_inc(job_dve, 1)
            prepared(dve)

            def row_factors(n, u):
                dve.wait_ge(xrn_ready, n + 1)
                if not before(n, 2):
                    dve.wait_ge(e_ready, (n - 1) * NG)
                nc.vector.reciprocal(row_n[:, u:u + 1], x_rn[:, u:u + 1]).then_inc(rown_ready, 1)
                dve.wait_ge(rown_ready, n + 1)
                ts(row_c[:, u:u + 1], row_n[:, u:u + 1], F(C1)).then_inc(rowc_ready, 1)
                ts(row_ip[:, u:u + 1], row_n[:, u:u + 1], F(C2)).then_inc(rowc_ready, 1)

            def x_low(n):
                dve.wait_ge(xT_hi, n + 1)
                low_part(xT[:, LO], ps_m[:, 0:C].rearrange("p (c s) -> p c s", c=CC), X_UP, xT[:, HI]
                         ).then_inc(xT_lo, 1)

            def q_low(n):
                dve.wait_ge(q_hi, n + 1)
                low_part(q_hl[:, LO, :], ps_m[:, 0:C], Q_DOWN, q_hl[:, HI, :]).then_inc(q_lo, 1)

            def maxima(i, par, g, u):
                dve.wait_ge(scores, i + 1)
                src = ps[:, BANK_B:BANK_B + 2, 0:2 * TA].rearrange("p b (h t) -> p b h t", h=2)
                nc.vector.tensor_reduce(s_max[:, par, :].rearrange("p (b h) -> p b h", b=2),
                                        src[:, :, :, 0:T], axis=AX_X, op=ALU.max).then_inc(max_ready, 1)
                dve.wait_ge(max_ready, i + 1)
                ts(s_bias[:, par, :], s_max[:, par, :], row_c[:, u:u + 1], -1.0).then_inc(bias_ready, 1)

            def e_low(i, par):
                dve.wait_ge(eT_hi, i + 1)
                low_part(eT[:, par, LO, :], ps[:, BANK_T, :], P_UP, eT[:, par, HI, :]).then_inc(eT_lo, 1)

            def group_dots(i, g, u):
                dve.wait_ge(prod, i + 1)
                for j in range(HG):
                    lo = (j % 2) * W + W_G
                    last = nc.vector.tensor_tensor_reduce(
                        out=e[:, g, j, :], in0=ps[:, BANK_N + j // 2, lo:lo + T], in1=e[:, g, j, :],
                        scale=1.0, scalar=0.0, op0=ALU.mult, op1=ALU.add,
                        accum_out=ege[:, u, g * HG + j:g * HG + j + 1])
                last.then_inc(dots, 1)

            CH = 6

            def tail_a(n, u):
                z = stats[:, u, :, W_Z]
                dve.wait_ge(stats_ready, (n + 1) * NG)
                dve.wait_ge(ip_ready, (n + 1) * NG)
                if not before(n, 1):
                    dve.wait_ge(text_ready, n)
                nc.vector.tensor_tensor(z_sq, z, z, ALU.mult).then_inc(chain, 1)
                nc.vector.tensor_copy(ip_kept, ip_score[:, u]).then_inc(ip_kept_ready, 1)
                nc.vector.reciprocal(z_inv, z).then_inc(z_link, 1)
                dve.wait_ge(chain, n * CH + 1)
                dve.wait_ge(dots, (n + 1) * NG)
                nc.vector.scalar_tensor_tensor(out=n_sq, in0=z_sq, scalar=F(GSC), in1=ege[:, u, :],
                                               op0=ALU.mult, op1=ALU.max).then_inc(nsq_ready, 1)
                dve.wait_ge(z_link, n + 1)
                ts(z_rho, z_inv, F(RHO)).then_inc(z_ready, 1)

            def tail_b(n, u):
                dve.wait_ge(ninv_ready, 2 * n + 2)
                nc.vector.tensor_tensor(sem_raw, stats[:, u, :, W_A:W_Z],
                                        repeated(n_inv.rearrange("p (h a) -> p h a", a=1), 2, NIP), ALU.mult
                                        ).then_inc(chain, 1)
                dve.wait_ge(chain, n * CH + 2)
                dve.wait_ge(ip_kept_ready, n + 1)
                nc.vector.scalar_tensor_tensor(out=fused, in0=sem_raw, scalar=SEM_SCALE * 2.0 ** -14,
                                               in1=ip_kept, op0=ALU.mult, op1=ALU.add
                                               ).then_inc(chain, 1)
                dve.wait_ge(chain, n * CH + 3)
                nc.vector.tensor_reduce(f_max, fused, axis=AX_X, op=ALU.max).then_inc(chain, 1)
                dve.wait_ge(chain, n * CH + 4)
                nc.vector.tensor_tensor(f_diff, fused, repeated(f_max.rearrange("p (h a) -> p h a", a=1), 2, NIP),
                                        ALU.subtract).then_inc(diff_ready, 1)

            def tail_c(n, col):
                dve.wait_ge(eip_ready, n + 1)
                nc.vector.reduce_sum(ip_sum, e_ip, AX_X).then_inc(chain, 1)
                dve.wait_ge(chain, n * CH + 5)
                nc.vector.reciprocal(ip_inv, ip_sum).then_inc(chain, 1)
                dve.wait_ge(chain, n * CH + 6)
                ts(ip_w, ip_inv, mask_sb[:, col], P_UP).then_inc(ipw_ready, 1)
                dve.wait_ge(ipw_ready, n + 1)
                if not before(n, 1):
                    dve.wait_ge(oT_psum, n)
                nc.vector.tensor_tensor(
                    p_ip[:, 0:NHN].rearrange("p (h n) -> p h n", n=NIP), e_ip,
                    repeated(ip_w.rearrange("p (h a) -> p h a", a=1), 2, NIP), ALU.mult
                ).then_inc(pip_ready, 1)

            def out_low(n):
                dve.wait_ge(oT_hi, n + 1)
                nc.vector.tensor_tensor(oT[:, LO], ps_m[:, 0:C + P].rearrange("p (c s) -> p c s", c=CC + 1),
                                        oT[:, HI], ALU.subtract).then_inc(oT_lo, 1)

            def add_residual(n, u):
                dve.wait_ge(y_psum, 2 * (n + 1))
                dve.wait_ge(res_ready, n + 1)
                if not before(n, 2):
                    dve.wait_ge(st_y[u], (n - u) * 8)
                nc.vector.scalar_tensor_tensor(
                    out=y[:, u, :].rearrange("p (b n) -> p b n", b=2), in0=ps[:, BANK_M:BANK_M + 2, 0:HALF],
                    scalar=F(YM), in1=x_res[:, u, :].rearrange("p (b n) -> p b n", b=2),
                    op0=ALU.mult, op1=ALU.add).then_inc(y_ready, 1)

            dve.wait_ge(pip_zero, 1)
            for n in range(2):
                row_factors(n, n)
            for n in range(2):
                x_low(n)
                q_low(n)
            dve.wait_ge(rowc_ready, 4)
            maxima(0, 0, 0, 0)
            for n, u, b, _f in tiles(dve):
                for g in range(NG):
                    i = n * NG + g
                    par = (u * NG + g) % 2
                    if not (known(i) and i == NT * NG - 1):
                        if g == NG - 1:
                            dve.wait_ge(rowc_ready, 2 * n + 4)
                        maxima(i + 1, 1 - par, (g + 1) % NG, u if g < NG - 1 else 1 - u)
                    if g == 0 and not before(n, 1) and not (known(n) and n + 1 >= NT):
                        q_low(n + 1)
                    if g == 1 and not before(n, 2):
                        out_low(n - 2)
                    if g == 3 and not before(n, 2):
                        add_residual(n - 2, u)
                    if g == 4 and loads_ahead(n):
                        x_low(n + 2)
                    e_low(i, par)
                    if g == 1 and not before(n, 1):
                        tail_a(n - 1, 1 - u)
                    if not (known(i) and i < 1):
                        group_dots(i - 1, (g - 1) % NG, u if g >= 1 else 1 - u)
                    if g == 4 and not before(n, 1):
                        tail_b(n - 1, 1 - u)
                    if g == 4 and not before(n, 1):
                        within = (n - 1) % TPB if known(n) else n - 1 - b * TPB
                        tail_c(n - 1, bass.ds(within, 1))
                    if g == 4 and loads_ahead(n):
                        row_factors(n + 2, u)
            n = NT - 1
            group_dots(NT * NG - 1, NG - 1, 1)
            out_low(n - 1)
            add_residual(n - 1, 0)
            tail_a(n, 1)
            tail_b(n, 1)
            tail_c(n, bass.ds(TPB - 1, 1))
            out_low(n)
            add_residual(n, 1)

        PASSES = ((HI, HI), (HI, LO), (LO, HI))

        @block.tensor
        def _(pe):
            pe.wait_ge(ident_ready, 2)
            pe.wait_ge(ld_ctx, 32 * B)

            def run_job(k):
                kind, a, h, _ = jobs[k]
                bank = ps[:, k % 4, :]
                if k >= 4:
                    emptied(pe, k - 4)
                if kind == "ctxT":
                    if k == 0:
                        pe.wait_ge(ip_nrm_ready, 1)
                    cols = slice(a * P, (a + 1) * P)
                    parts = [(ctx_main[:, b, cols], P * b) for b in range(B)]
                    parts += [(ctx_rest[:, cols], C_REST), (ip_raw[:, cols], C_IP), (ip_nrm[:, cols], C_IPN)]
                    for src, lo in parts:
                        n = src.shape[0]
                        last = nc.tensor.transpose(bank[:, lo:lo + n], src, ident[0:n, 0:n])
                    return last
                if kind == "mask":
                    pe.wait_ge(ld_small, 32)
                    return nc.tensor.transpose(bank[:, 0:TPB], mask_rows, ident[0:TPB, 0:TPB])
                if kind == "wv":
                    pe.wait_ge(ld_out, 16)
                    emptied(pe, job_at("vip")[0])
                    for c in range(CC):
                        last = nc.tensor.matmul(bank[:, 0:HALF], vip_blk[:, a, c * NHN:c * NHN + P],
                                                wo_sb[:, c, h * HALF:(h + 1) * HALF],
                                                start=(c == 0), stop=(c == CC - 1))
                    return last
                if k == job_at("kT")[0]:
                    for c in range(EC):
                        emptied(pe, c)
                load = {"kT": ld_k, "kip": ld_kip, "vip": ld_vip, "v": ld_v, "v_rest": ld_v}.get(kind)
                if load:
                    pe.wait_ge(load, 16)
                if kind in ("kip", "vip"):
                    slot = 0 if kind == "kip" else 1
                    for g in range(CC):
                        for c in range(EC):
                            last = nc.tensor.matmul(
                                bank[:, g * B * NIP:(g + 1) * B * NIP],
                                w_stage[:, slot, c, g * P:(g + 1) * P], ctxT[:, c, C_IP:C_IPN],
                                start=(g == 0 and c == 0), stop=(c == EC - 1), skip_group_check=True)
                    return last
                for c in range(EC):
                    first, stop = c == 0, c == EC - 1
                    if kind == "kT":
                        last = nc.tensor.matmul(bank[:, 0:C_IP], w_stage[:, 0, c, a * P:(a + 1) * P],
                                                ctxT[:, c, 0:C_IP], start=first, stop=stop)
                    elif kind == "g":
                        last = nc.tensor.matmul(bank[:, 0:C_ALL], ctxT[:, c, a * P:(a + 1) * P],
                                                ctxT[:, c, :], start=first, stop=stop)
                    elif kind == "g_rest":
                        last = nc.tensor.matmul(bank[0:B * 32, 0:C_ALL - C_REST],
                                                ctxT[:, c, C_REST:C_IP], ctxT[:, c, C_REST:C_ALL],
                                                start=first, stop=stop)
                    elif kind == "v":
                        last = nc.tensor.matmul(bank[:, 0:HALF], ctxT[:, c, a * P:(a + 1) * P],
                                                w_stage[:, 1, c, h * HALF:(h + 1) * HALF],
                                                start=first, stop=stop)
                    else:
                        last = nc.tensor.matmul(bank[0:B * 32, 0:HALF], ctxT[:, c, C_REST:C_IP],
                                                w_stage[:, 1, c, a * HALF:(a + 1) * HALF],
                                                start=first, stop=stop)
                return last

            def transpose_x(n):
                pe.wait_ge(xhat_ready, n + 1)
                for c in range(CC):
                    last = nc.tensor.transpose(ps_m[:, c * P:(c + 1) * P], x_hat[:, c * P:(c + 1) * P], ident[:])
                last.then_inc(xT_psum, 1)

            def queries(n, chunks):
                if 0 in chunks:
                    pe.wait_ge(xT_lo, n + 1)
                for k in chunks:
                    for w_part, x_part in PASSES:
                        for c in range(CC):
                            first = (w_part, x_part) == PASSES[0] and c == 0
                            final = (w_part, x_part) == PASSES[-1] and c == CC - 1
                            last = nc.tensor.matmul(
                                ps_m[:, k * P:(k + 1) * P], wq_hl[:, w_part, c, k * P:(k + 1) * P],
                                xT[:, x_part, c, :], start=(first and k in (0, 4)), stop=final,
                                skip_group_check=True)
                if chunks[-1] == CC - 1:
                    last.then_inc(q_psum, 1)

            def group_scores(i, g, u, b):
                for j in range(HG):
                    last = nc.tensor.matmul(ps[:, BANK_B + j // 2, (j % 2) * TA:(j % 2 + 1) * TA],
                                            q_stack[:, u, j, g * P:(g + 1) * P], k_tab[:, b, j, g, :],
                                            start=(j % 2 == 0), stop=True, skip_group_check=True)
                last.then_inc(scores, 1)

            def transpose_out(n):
                pe.wait_ge(text_ready, n + 1)
                pe.wait_ge(pip_ready, n + 1)
                for c in range(CC):
                    nc.tensor.transpose(ps_m[:, c * P:(c + 1) * P], text[:, c * HG:(c + 1) * HG, :], ident[:])
                nc.tensor.transpose(ps_m[:, C:C + P], p_ip, ident[:]).then_inc(oT_psum, 1)

            def output_product(n, h, b):
                cols = slice(h * HALF, (h + 1) * HALF)
                dst = ps[:, BANK_M + h, 0:HALF]
                for o_part, w_part in PASSES:
                    if h == 0 and (o_part, w_part) == PASSES[0]:
                        pe.wait_ge(oT_lo, n + 1)
                    for c in range(CC):
                        nc.tensor.matmul(dst, oT[:, o_part, c, :], wo_hl[:, w_part, c, cols],
                                         start=((o_part, w_part) == PASSES[0] and c == 0), stop=False)
                    last = nc.tensor.matmul(dst, oT[:, o_part, CC, :], wv_hl[:, w_part, b, cols],
                                            start=False, stop=((o_part, w_part) == PASSES[-1]))
                last.then_inc(y_psum, 1)

            def main_product(i, par, g, b):
                pe.wait_ge(eT_hi, i + 1)
                pe.wait_ge(rT_ready, i + 1)
                if not (known(i) and i < 1):
                    pe.wait_ge(stats_ready, i)
                for pr in range(2):
                    for e_part, t_part in PASSES:
                        if pr == 0 and e_part == LO:
                            pe.wait_ge(eT_lo, i + 1)
                        for hh in range(2):
                            j = 2 * pr + hh
                            nc.tensor.matmul(ps[:, BANK_N + pr, hh * W:(hh + 1) * W],
                                             eT[:, par, e_part, j * P:(j + 1) * P],
                                             t_main[:, t_part, b, g * HG + j, :],
                                             start=(hh == 0 and (e_part, t_part) == PASSES[0]), stop=False,
                                             skip_group_check=True)
                    dst = ps[:, BANK_N + pr, 0:2 * W].rearrange("p (h w) -> p h w", h=2)[:, :, 0:WR]
                    for t_part in range(2):
                        last = nc.tensor.matmul(dst, rT[:, par, pr, :], t_rest[:, t_part, b, 2 * g + pr],
                                                start=False, stop=(t_part == 1), skip_group_check=True)
                last.then_inc(prod, 1)

            def transpose_main(i, g):
                if not (known(i) and i < 1):
                    pe.wait_ge(eT_lo, i)
                for j in range(HG):
                    last = nc.tensor.transpose(ps[:, BANK_T, j * P:(j + 1) * P], e[:, g, j, TR:T], ident[:])
                last.then_inc(eT_psum, 1)

            def transpose_rest(i):
                pe.wait_ge(rest_lo, i + 1)
                for pr in range(2):
                    last = nc.tensor.transpose(
                        ps[:, BANK_T + 1, pr * P // 2:(pr + 1) * P // 2].bitcast(F16),
                        e_rest[:, pr].rearrange("p a h t -> p (a h t)"), ident16[:])
                last.then_inc(rT_psum, 1)

            for k in range(len(jobs)):
                run_job(k).then_inc(job_done, 1)
            prepared(pe)
            for n in range(2):
                if n:
                    pe.wait_ge(q_lo, n)
                transpose_x(n)
                queries(n, range(CC))
            pe.wait_ge(ld_qs[0], 256)
            pe.wait_ge(q_lo, 2)
            group_scores(0, 0, 0, 0)
            for n, u, b, first_pair in tiles(pe):
                for g in range(NG):
                    i = n * NG + g
                    par = (u * NG + g) % 2
                    pe.wait_ge(ip_ready, i + 1)
                    pe.wait_ge(e_ready, i + 1)
                    if not (known(i) and i == NT * NG - 1):
                        nb = b
                        if g == NG - 1:
                            pe.wait_ge(ld_qs[1 - u], (n + u + 2) * 128)
                            if known(n):
                                nb = (n + 1) // TPB
                        group_scores(i + 1, (g + 1) % NG, u if g < NG - 1 else 1 - u, nb)
                    transpose_main(i, g)
                    if not (known(i) and i < 1):
                        pb = b - 1 if first_pair and b and u == 0 and g == 0 else b
                        main_product(i - 1, 1 - par, (g - 1) % NG, pb)
                    transpose_rest(i)
                    if g == 0 and not before(n, 2):
                        if known(n) and n + 1 >= NT:
                            pe.wait_ge(y_ready, n - 2)
                        else:
                            pe.wait_ge(q_lo, n + 2)
                        transpose_out(n - 2)
                    if g in (1, 2) and not before(n, 2):
                        output_product(n - 2, g - 1, b - 1 if first_pair and b else b)
                    if g == 3 and loads_ahead(n):
                        if not before(n, 2):
                            pe.wait_ge(y_ready, n - 1)
                        elif n == 1:
                            pe.wait_ge(q_lo, 3)
                        transpose_x(n + 2)
                    if g == 4 and loads_ahead(n):
                        queries(n + 2, range(CC))
            main_product(NT * NG - 1, 1, NG - 1, B - 1)
            for n in (NT - 2, NT - 1):
                pe.wait_ge(y_ready, n)
                transpose_out(n)
                output_product(n, 0, B - 1)
                output_product(n, 1, B - 1)


_INS = ["x", "ctx_2048", "fside_S_0", "L0_xattn_W_q", "L0_xattn_W_k", "L0_xattn_W_v",
        "L0_xattn_W_k_ip", "L0_xattn_W_v_ip", "L0_xattn_W_out", "L0_xattn_b_out"]


def kernel(**inputs):
    import numpy as np
    import concourse.bacc as bacc
    from concourse.bass_utils import run_bass_kernel_spmd

    nc = bacc.Bacc("TRN2", target_bir_lowering=False, num_devices=1)
    arrays, args = {}, []
    for name in _INS:
        a = np.ascontiguousarray(inputs[name])
        arrays[f"in_{name}"] = a
        args.append(nc.dram_tensor(f"in_{name}", a.shape, mybir.dt.from_np(a.dtype),
                                   kind="ExternalInput").ap())
    shape = tuple(inputs["x"].shape)
    out = nc.dram_tensor("out", shape, F32, kind="ExternalOutput").ap()
    xattn_program(nc, *args, out)
    got = run_bass_kernel_spmd(nc, [arrays], core_ids=[0])
    return got.results[0]["out"]
```

```python
from contextlib import ExitStack

import concourse.bass as bass
from concourse import mybir

F32 = mybir.dt.float32
F16 = mybir.dt.float16
ACT = mybir.ActivationFunctionType
ALU = mybir.AluOpType
AX_X = mybir.AxisListType.X

P = 128
HEADS = 20
NIP = 4
EPS = 1e-12
SEM_SCALE = 0.5

BANK_B, BANK_T, BANK_N, BANK_M = 0, 2, 4, 6


def repeated(ap, axis, n):
    shape = list(ap.shape)
    shape[axis] = n
    return ap.broadcast_to(shape)


def xattn_program(nc, x, ctx, mask, w_q, w_k, w_v, w_k_ip, w_v_ip, w_out, b_out, out):
    B, S, C = x.shape
    TA, E = ctx.shape[1:]
    T = TA - NIP
    TR = T - P
    D = C // HEADS
    SCALE = float(D) ** -0.5
    CC = C // P
    EC = E // P
    HG = P // D
    NG = HEADS // HG
    NPR = HEADS // 2
    TPB = S // P
    NT = B * TPB
    HALF = C // 2
    NHN = HEADS * NIP
    W = D + NIP + 1 + T
    W_A, W_Z, W_G = D, D + NIP, D + NIP + 1
    WR = W_G + TR
    HI, LO = 0, 1
    assert D == 32 and NG == CC == 5 and 0 < TR <= D and TA * 2 <= 512 and W * 2 <= 512

    C_REST, C_IPN = P, P + 32
    C_B = C_IPN + NIP
    C_IP = B * C_B
    C_ALL = C_IP + B * NIP

    x_t = x.rearrange("b (t p) c -> (b t) p c", p=P)
    out_t = out.rearrange("b (t p) c -> (b t) p c", p=P)

    with ExitStack() as stack:
        def sb(name, shape, dt=F32):
            return stack.enter_context(nc.sbuf_tensor(name, shape, dt))

        def sem(name):
            return stack.enter_context(nc.semaphore(name))

        ps = stack.enter_context(nc.psum_tensor("ps", [P, 8, 512], F32))
        ps_m = ps[:, BANK_M:BANK_M + 2, :].rearrange("p b n -> p (b n)")

        ident = sb("ident", [P, P])
        ident16 = sb("ident16", [P, P], F16)
        minus_half = sb("minus_half", [P, HEADS])
        tiny = sb("tiny", [P, 1])
        p_up = sb("p_up", [P, 1])
        wq_hl = sb("wq_hl", [P, 2, CC, C], F16)
        wo_hl = sb("wo_hl", [P, 2, CC, C], F16)
        wv_hl = sb("wv_hl", [P, 2, B, C], F16)
        mask_sb = sb("mask_sb", [P, TPB])
        bias_sb = sb("bias_sb", [P, C])
        k_tab = sb("k_tab", [P, HG, B, NG, TA], F16)
        t_main = sb("t_main", [P, 2, B, HEADS, W], F16)
        t_rest = sb("t_rest", [P, 2, B, NPR, 2, WR], F16)
        x_in = sb("x_in", [P, 2, C])
        x_sq, x_sqg, x_rn, row_n, row_c, row_ip = (
            sb(n, [P, 2]) for n in ("x_sq", "x_sqg", "x_rn", "row_n", "row_c", "row_ip"))
        ip_pick = sb("ip_pick", [P, B * NIP])
        fac = sb("fac", [P, 32])
        mx = sb("mx", [P, 16])

        AREA = 29200
        area = sb("area", [P, AREA])
        cut = [0]

        def part(rows, *dims, dt=F32):
            n = 1
            for d in dims:
                n *= d
            words = n if dt == F32 else (n + 1) // 2
            view = area[0:rows, cut[0]:cut[0] + words]
            cut[0] += words
            assert cut[0] <= AREA
            if dt != F32:
                view = view.bitcast(dt)
            if len(dims) == 1:
                return view
            names = "abcd"[:len(dims)]
            return view.rearrange(f"p ({' '.join(names)}) -> p {' '.join(names)}",
                                  **dict(zip(names[1:], dims[1:])))

        ctx_main = part(P, B, E)
        ctx_rest = part(B * 32, E)
        ip_raw = part(B * NIP, E)
        ip_nrm = part(B * NIP, E)
        cut_inputs = cut[0]
        ip_sq = part(B * NIP, 1)
        ip_sqg = part(B * NIP, 1)
        ip_rn = part(B * NIP, 1)
        ctxT = part(P, EC, C_ALL)
        mask_rows = part(TPB, P)
        vip_blk = part(P, B, CC * (NHN // CC + NHN))
        w_stage = part(P, 2, EC, C)
        wq_sb = part(P, CC, C)
        wo_sb = part(P, CC, C)
        k_nat = part(P, 2, B, NG, TA, dt=F16)
        g_nat = part(P, 2, B, W - D + 1, dt=F16)
        v_rest = part(P, 2, HALF, dt=F16)
        ip_parts = part(P, C)
        g_rest = part(B * 32, 2, WR - D + 1, dt=F16)

        cut[0] = 0
        x_hat = part(P, C)
        x_junk = part(P, C)
        xT = part(P, 2, CC, P, dt=F16)
        q_hl = part(P, 2, CC * P, dt=F16)
        q_stack = part(P, 2, HG, NG * P, dt=F16)
        assert cut[0] <= cut_inputs
        e = part(P, NG, HG, T)
        e_rest = part(P, 2, 2, 2, 32, dt=F16)
        rest_up = part(P, 2, 2, 32)
        eT = part(P, 2, 2, HG * P, dt=F16)
        rT = part(P, 2, 2, P, dt=F16)
        stats = part(P, 2, HEADS, W_G)
        text = part(P, HEADS, D)
        oT = part(P, 2, CC + 1, P, dt=F16)
        x_res = part(P, 2, C)
        y = part(P, 2, C)
        s_max = part(P, 2, HG)
        s_bias = part(P, 2, HG)
        ege = part(P, 2, HEADS)
        ip_score = part(P, 2, HEADS, NIP)
        ip_kept = part(P, HEADS, NIP)
        z_inv = part(P, HEADS)
        z_rho = part(P, HEADS)
        z_sq = part(P, HEADS)
        n_sq = part(P, HEADS)
        n_inv = part(P, HEADS)
        sem_raw = part(P, HEADS, NIP)
        fused = part(P, HEADS, NIP)
        f_max = part(P, HEADS)
        f_diff = part(P, HEADS, NIP)
        e_ip = part(P, HEADS, NIP)
        ip_sum = part(P, HEADS)
        ip_inv = part(P, HEADS)
        ip_w = part(P, HEADS)
        p_ip = part(P, P)

        (R_CTX, R_WK, R_WKI, R_WV, R_WVI, R_WQ, R_WO, KF, KIF, VF, AF, GF, G2F, WQF, WOF, C1, C2,
         RHO, WVF, YM, GSC, R_WVJ, SCR0, SCR1, SCR2, N_WVJ) = range(26)
        (N_CTX, N_WK, N_WKI, N_WV, N_WVI, N_WQ, N_WO, M0) = range(8)

        def F(k):
            return fac[:, k:k + 1]

        def N(k):
            return mx[:, k:k + 1]

        ld_ctx, ld_ip, ld_k, ld_v, ld_kip, ld_vip, ld_q, ld_out, ld_small = (
            sem(f"ld_{n}") for n in ("ctx", "ip", "k", "v", "kip", "vip", "q", "out", "small"))
        ld_k_head = sem("ld_k_head")
        pick_ready = sem("pick_ready")
        ip_stacked = sem("ip_stacked")
        ident_ready, zeroed, half_ready, ident_zero, ip_sq_ready, ip_guard, ip_rn_ready, ip_nrm_ready = (
            sem(n) for n in ("ident_ready", "zeroed", "half_ready", "ident_zero", "ip_sq_ready",
                             "ip_guard", "ip_rn_ready", "ip_nrm_ready"))
        part_max, all_max, fac_link, fac_ready = (
            sem(n) for n in ("part_max", "all_max", "fac_link", "fac_ready"))
        job_done, job_act, job_dve = sem("job_done"), sem("job_act"), sem("job_dve")
        wsplit_hi, wsplit_lo, k_stacked, tables_ready = (
            sem(n) for n in ("wsplit_hi", "wsplit_lo", "k_stacked", "tables_ready"))
        ld_x = [sem("ld_x0"), sem("ld_x1")]
        ld_qs = [sem("ld_qs0"), sem("ld_qs1")]
        ld_res = [sem("ld_res0"), sem("ld_res1")]
        st_y = [sem("st_y0"), sem("st_y1")]
        xsq_ready, xsq_guard, xrn_ready, xhat_ready, rown_ready, rowc_ready = (
            sem(n) for n in ("xsq_ready", "xsq_guard", "xrn_ready", "xhat_ready", "rown_ready", "rowc_ready"))
        xT_psum, xT_hi, xT_lo = (sem(n) for n in ("xT_psum", "xT_hi", "xT_lo"))
        q_psum, q_hi, q_lo = ([sem(n + "_0123"), sem(n + "_4")] for n in ("q_psum", "q_hi", "q_lo"))
        scores, max_ready, bias_ready, e_ready, rest_scaled, rest_hi, rest_lo = (
            sem(n) for n in ("scores", "max_ready", "bias_ready", "e_ready", "rest_scaled", "rest_hi",
                             "rest_lo"))
        eT_psum, rT_psum, eT_hi, eT_lo, rT_ready, prod, stats_ready, dots = (
            sem(n) for n in ("eT_psum", "rT_psum", "eT_hi", "eT_lo", "rT_ready", "prod", "stats_ready", "dots"))
        z_link, z_ready, text_ready, nsq_ready, ninv_ready, chain = (
            sem(n) for n in ("z_link", "z_ready", "text_ready", "nsq_ready", "ninv_ready", "chain"))
        ip_kept_ready, ip_ready = sem("ip_kept_ready"), sem("ip_ready")
        diff_ready, eip_ready, ipw_ready, pip_ready, pip_zero = (
            sem(n) for n in ("diff_ready", "eip_ready", "ipw_ready", "pip_ready", "pip_zero"))
        oT_psum, oT_hi, oT_lo, y_psum, res_ready = (
            sem(n) for n in ("oT_psum", "oT_hi", "oT_lo", "y_psum", "res_ready"))
        y_ready = [sem("y_ready_0"), sem("y_ready_1")]

        block = stack.enter_context(nc.Block())

        jobs = [("ctxT", c, 0, "act" if c % 2 else "dve") for c in range(EC)]
        jobs += [("kT", g, 0, "both") for g in range(NG)]
        jobs += [("v", b, h, "both") for b in range(B) for h in range(2)]
        jobs += [("v_rest", 0, 0, "both")]
        jobs += [("kip_part", h, 0, "act") for h in range(2)] + [("kip", 0, 0, "both")]
        jobs += [("g", b, 0, "both") for b in range(B)] + [("g_rest", 0, 0, "both")]
        jobs += [("mask", 0, 0, "act")]
        jobs += [("vip_part", h, 0, "act") for h in range(2)] + [("vip", 0, 0, "act")]
        jobs += [("wv", b, h, "both") for b in range(B) for h in range(2)]

        def job_at(kind):
            return [k for k, j in enumerate(jobs) if j[0] == kind]

        BESIDE = {job_at("kip_part")[0]: ("x", 0), job_at("kip")[0]: ("q", 0), job_at("g_rest")[0]: ("x", 1),
                  job_at("wv")[0]: ("q", 1)}

        def inputs_read(eng):
            eng.wait_ge(job_done, EC)
            eng.wait_ge(part_max, 1)
            eng.wait_ge(ip_nrm_ready, 1)

        def by_act(k):
            return sum(j[3] in ("act", "both") for j in jobs[:k + 1])

        def by_dve(k):
            return sum(j[3] in ("dve", "both") for j in jobs[:k + 1])

        def emptied(eng, k):
            if jobs[k][3] == "act":
                eng.wait_ge(job_act, by_act(k))
            else:
                eng.wait_ge(job_dve, by_dve(k))

        def prepared(eng):
            eng.wait_ge(job_done, len(jobs))
            eng.wait_ge(job_act, by_act(len(jobs) - 1))
            eng.wait_ge(job_dve, by_dve(len(jobs) - 1))
            eng.wait_ge(wsplit_lo, 2)
            eng.wait_ge(tables_ready, 2)
            eng.wait_ge(k_stacked, 16 * 4 * HG)
            eng.wait_ge(ip_stacked, 2)

        NP, PPB = NT // 2, TPB // 2
        SEGMENTS = []
        for b in range(B):
            lo, hi = b * PPB, (b + 1) * PPB
            SEGMENTS += [(lo, lo + 1, b), (lo + 1, hi - 1, b), (hi - 1, hi, b)]

        def tiles(eng):
            for lo, hi, b in SEGMENTS:
                if hi - lo == 1:
                    for u in range(2):
                        yield lo * 2 + u, u, b, lo == b * PPB
                else:
                    with eng.Fori(lo, hi) as pair:
                        for u in range(2):
                            yield pair * 2 + u, u, b, False

        def known(n):
            return isinstance(n, int)

        def before(n, k):
            return known(n) and n < k

        def residual_added(eng, count):
            for half in range(2):
                eng.wait_ge(y_ready[half], count)

        def loads_ahead(n):
            return not known(n) or n + 2 < NT

        @block.sync
        def _(sp):
            for b in range(B):
                sp.dma_start(ip_raw[b * NIP:(b + 1) * NIP, :], ctx[b, T:TA, :]).then_inc(ld_ip, 16)
            for b in range(B):
                sp.dma_start(ctx_main[:, b, :], ctx[b, TR:T, :]).then_inc(ld_ctx, 16)
                sp.dma_start(ctx_rest[b * 32:b * 32 + 32, :], ctx[b, 0:32, :]).then_inc(ld_ctx, 16)
            w_k_chunks = w_k.rearrange("(c p) n -> p c n", p=P)
            sp.dma_start(w_stage[:, 0, 0:EC // 2], w_k_chunks[:, 0:EC // 2]).then_inc(ld_k_head, 16)
            sp.dma_start(w_stage[:, 0, EC // 2:EC], w_k_chunks[:, EC // 2:EC]).then_inc(ld_k, 16)
            sp.dma_start(w_stage[:, 1], w_v.rearrange("(c p) n -> p c n", p=P)).then_inc(ld_v, 16)
            def load_x(n, u):
                sp.dma_start(x_in[:, u, :], x_t[n]).then_inc(ld_x[u], 16)

            load_x(0, 0)
            load_x(1, 1)
            sp.dma_start(wq_sb, w_q.rearrange("(c p) n -> p c n", p=P)).then_inc(ld_q, 16)
            sp.dma_start(wo_sb, w_out.rearrange("(c p) n -> p c n", p=P)).then_inc(ld_out, 16)
            sp.dma_start(mask_rows, mask.rearrange("(t p) -> t p", p=P)).then_inc(ld_small, 16)
            sp.dma_start(bias_sb[:], repeated(b_out.rearrange("(a n) -> a n", a=1), 0, P)
                         ).then_inc(ld_small, 16)

            sp.wait_ge(job_done, job_at("kT")[-1] + 1)
            sp.wait_ge(part_max, 2)
            sp.dma_start(w_stage[:, 0], w_k_ip.rearrange("(c p) n -> p c n", p=P)).then_inc(ld_kip, 16)
            sp.wait_ge(job_dve, by_dve(job_at("kT")[-1]))
            for hl in range(2):
                for j in range(HG):
                    for k in (hl, 2 + hl):
                        sp.dma_start(k_tab[32 * k:32 * k + 32, j, :, :, 0:T],
                                     k_nat[32 * j:32 * j + 32, hl, :, :, 0:T]).then_inc(k_stacked, 16)
            sp.wait_ge(job_done, job_at("v_rest")[-1] + 1)
            sp.wait_ge(part_max, 3)
            sp.dma_start(w_stage[:, 1], w_v_ip.rearrange("(c p) n -> p c n", p=P)).then_inc(ld_vip, 16)
            def stack_queries(n, u):
                if not before(n, 2):
                    sp.wait_ge(scores, (n - 1) * NG)
                for bank in range(2):
                    sp.wait_ge(q_hi[bank], n + 1)
                    sp.wait_ge(q_lo[bank], n + 1)
                for hl in range(2):
                    for j in range(HG):
                        for k in (2 * hl, 2 * hl + 1):
                            sp.dma_start(q_stack[32 * k:32 * k + 32, u, j, :],
                                         q_hl[32 * j:32 * j + 32, hl, :]).then_inc(ld_qs[u], 16)

            inputs_read(sp)
            stack_queries(0, 0)
            stack_queries(1, 1)
            prepared(sp)
            for n, u, _b, _f in tiles(sp):
                if loads_ahead(n):
                    sp.wait_ge(xhat_ready, n + 1)
                    load_x(n + 2, u)
                if not before(n, 1):
                    if not before(n, 3):
                        residual_added(sp, n - 2)
                    sp.dma_start(x_res[:, 1 - u, :], x_t[n - 1]).then_inc(ld_res[1 - u], 16)
                    if not (known(n) and n + 1 >= NT):
                        stack_queries(n + 1, 1 - u)
                if not before(n, 2):
                    residual_added(sp, n - 1)
                    sp.dma_start(out_t[n - 2], y[:, u, :]).then_inc(st_y[u], 16)
            residual_added(sp, NT - 2)
            sp.dma_start(x_res[:, 1, :], x_t[NT - 1]).then_inc(ld_res[1], 16)
            for n in (NT - 2, NT - 1):
                residual_added(sp, n + 1)
                sp.dma_start(out_t[n], y[:, n % 2, :]).then_inc(st_y[n % 2], 16)
            for k in range(2):
                sp.wait_ge(st_y[k], 16 * NT // 2)

        @block.gpsimd
        def _(pool):
            nc.gpsimd.memset(ident[:], 0.0).then_inc(ident_zero, 1)
            pool.wait_ge(ident_zero, 1)
            nc.gpsimd.affine_select(out=ident[:], in_=ident[:], compare_op=ALU.not_equal, fill=1.0,
                                    base=0, pattern=[[-1, P]], channel_multiplier=1
                                    ).then_inc(ident_ready, 1)
            nc.gpsimd.memset(minus_half[:], -0.5).then_inc(half_ready, 1)
            nc.gpsimd.memset(tiny[:], 1e-36).then_inc(half_ready, 1)
            nc.gpsimd.memset(p_up[:], 2.0 ** 14).then_inc(half_ready, 1)
            nc.gpsimd.memset(ip_pick[:], 0.0).then_inc(pick_ready, 1)
            for q in range(4):
                pool.wait_ge(pick_ready, 1 + q)
                nc.gpsimd.affine_select(out=ip_pick[:], in_=ip_pick[:], compare_op=ALU.not_equal, fill=1.0,
                                        base=-(32 * q + 32 - B * NIP), pattern=[[-1, B * NIP]],
                                        channel_multiplier=1).then_inc(pick_ready, 1)
            pool.wait_ge(ident_ready, 1)
            nc.gpsimd.tensor_copy(ident16[:], ident[:]).then_inc(ident_ready, 1)
            pool.wait_ge(ip_guard, 1)
            pool.wait_ge(half_ready, 3)
            nc.gpsimd.tensor_tensor(ip_rn, ip_sqg, minus_half[0:B * NIP, 0:1], ALU.pow
                                    ).then_inc(ip_rn_ready, 1)

            def unit_rows(n, u):
                pool.wait_ge(xsq_ready, n + 1)
                nc.gpsimd.tensor_tensor(x_sqg[:, u:u + 1], x_sq[:, u:u + 1], tiny[:], ALU.add
                                        ).then_inc(xsq_guard, 1)
                pool.wait_ge(xsq_guard, n + 1)
                if not before(n, 2):
                    pool.wait_ge(rown_ready, n - 1)
                nc.gpsimd.tensor_tensor(x_rn[:, u:u + 1], x_sqg[:, u:u + 1], minus_half[:, 0:1], ALU.pow
                                        ).then_inc(xrn_ready, 1)
                pool.wait_ge(xrn_ready, n + 1)
                if not before(n, 1):
                    pool.wait_ge(xT_psum, n)
                nc.gpsimd.tensor_tensor(x_hat, x_in[:, u, :], repeated(x_rn[:, u:u + 1], 1, C), ALU.mult
                                        ).then_inc(xhat_ready, 1)

            def across(k, m):
                pool.wait_ge(part_max, k + 1)
                nc.gpsimd.partition_all_reduce(N(m), N(M0 + m), P, bass.bass_isa.ReduceOp.max
                                               ).then_inc(all_max, 1)

            across(0, N_CTX)
            across(1, N_WK)
            nc.gpsimd.memset(t_rest[:], 0.0).then_inc(zeroed, 1)
            across(2, N_WV)
            nc.gpsimd.memset(vip_blk, 0.0).then_inc(zeroed, 1)
            for hl in range(2):
                one = 1.0 if hl == HI else 0.0
                nc.gpsimd.memset(g_nat[:, hl, :, NIP:NIP + 1], one).then_inc(zeroed, 1)
                nc.gpsimd.memset(g_rest[:, hl, NIP:NIP + 1], one).then_inc(zeroed, 1)
            inputs_read(pool)
            unit_rows(0, 0)
            across(3, N_WQ)
            across(4, N_WO)
            unit_rows(1, 1)
            across(5, N_WKI)
            across(6, N_WVI)
            prepared(pool)
            nc.gpsimd.memset(p_ip, 0.0).then_inc(pip_zero, 1)

            def norm_inverse(n, half):
                heads = slice(half * HEADS // 2, (half + 1) * HEADS // 2)
                pool.wait_ge(nsq_ready, n + 1)
                nc.gpsimd.tensor_tensor(n_inv[:, heads], n_sq[:, heads], minus_half[:, heads], ALU.pow
                                        ).then_inc(ninv_ready, 1)

            def text_part(n, u):
                pool.wait_ge(z_ready, n + 1)
                if not before(n, 1):
                    pool.wait_ge(oT_psum, n)
                nc.gpsimd.tensor_tensor(text, stats[:, u, :, 0:D],
                                        repeated(z_rho.rearrange("p (h a) -> p h a", a=1), 2, D), ALU.mult
                                        ).then_inc(text_ready, 1)

            def residual(n, u):
                pool.wait_ge(ld_res[u], (n - u + 2) * 8)
                nc.gpsimd.tensor_tensor(x_res[:, u, :], x_res[:, u, :], bias_sb[:], ALU.add
                                        ).then_inc(res_ready, 1)

            def split_rest(i, g):
                src = e[:, g, :, 0:32].rearrange("p (a h) t -> p a h t", a=2)
                up = repeated(repeated(repeated(p_up[:].rearrange("p (a h t) -> p a h t", a=1, h=1), 3, 32), 2, 2),
                              1, 2)
                pool.wait_ge(e_ready, i + 1)
                if not (known(i) and i < 1):
                    pool.wait_ge(rT_psum, i)
                nc.gpsimd.tensor_tensor(rest_up, src, up, ALU.mult).then_inc(rest_scaled, 1)
                nc.gpsimd.tensor_tensor(e_rest[:, :, HI], src, up, ALU.mult).then_inc(rest_hi, 1)
                pool.wait_ge(rest_scaled, i + 1)
                pool.wait_ge(rest_hi, i + 1)
                nc.gpsimd.tensor_tensor(e_rest[:, :, LO], rest_up, e_rest[:, :, HI], ALU.subtract
                                        ).then_inc(rest_lo, 1)

            for n, u, _b, _f in tiles(pool):
                for g in range(NG):
                    split_rest(n * NG + g, g)
                    if g == 1 and not before(n, 2):
                        residual(n - 2, u)
                    if g == 2 and loads_ahead(n):
                        unit_rows(n + 2, u)
                    if g == 2 and not before(n, 1):
                        text_part(n - 1, 1 - u)
                    last_tile = known(n) and n + 1 >= NT
                    if g == 2 and last_tile:
                        norm_inverse(n - 1, 0)
                        norm_inverse(n - 1, 1)
                    if g in (3, 4) and not before(n, 1) and not last_tile:
                        norm_inverse(n - 1, g - 3)
            residual(NT - 2, 0)
            norm_inverse(NT - 1, 0)
            norm_inverse(NT - 1, 1)
            text_part(NT - 1, 1)
            residual(NT - 1, 1)

        def empty(k, high, low, plain):
            kind, a, h, _ = jobs[k]
            bank = ps[:, k % 4, :]

            def both(dst, src, k, rows=slice(0, P)):
                f = fac[rows, k:k + 1]
                if high:
                    return high(dst(HI), src, f)
                return low(dst(LO), src, f, dst(HI))

            if kind == "ctxT":
                return plain(ctxT[:, a, :], bank[:, 0:C_ALL])
            if kind == "mask":
                return plain(mask_sb[:], bank[:, 0:TPB])
            if kind == "kT":
                src = bank[:, 0:B * C_IPN].rearrange("p (b w) -> p b w", b=B)
                both(lambda hl: k_nat[:, hl, :, a, 0:TR], src[:, :, C_REST:C_REST + TR], KF)
                return both(lambda hl: k_nat[:, hl, :, a, TR:T], src[:, :, 0:P], KF)
            if kind in ("kip_part", "vip_part"):
                return plain(ip_parts[:, a * HALF:(a + 1) * HALF], bank[:, 0:HALF])
            if kind == "kip":
                src = bank[:, 0:CC * B * NIP].rearrange("p (g n) -> p g n", g=CC)
                for b in range(B):
                    last = both(lambda hl: k_nat[:, hl, b, :, T:TA], src[:, :, b * NIP:(b + 1) * NIP], KIF)
                return last
            if kind == "g":
                both(lambda hl: g_nat[:, hl, a, 0:NIP], bank[:, C_IPN:C_B], AF)
                both(lambda hl: g_nat[:, hl, a, NIP + 1:NIP + 1 + TR], bank[:, C_REST:C_REST + TR], G2F)
                return both(lambda hl: g_nat[:, hl, a, NIP + 1 + TR:NIP + 1 + T], bank[:, 0:P], GF)
            if kind == "g_rest":
                r = slice(0, B * 32)
                both(lambda hl: g_rest[:, hl, 0:NIP], bank[r, 32:32 + NIP], AF, r)
                return both(lambda hl: g_rest[:, hl, NIP + 1:NIP + 1 + TR], bank[r, 0:TR], GF, r)
            if kind == "v":
                return both(lambda hl: t_main[:, hl, a, h * 10:h * 10 + 10, 0:D],
                            bank[:, 0:HALF].rearrange("p (n d) -> p n d", d=D), VF)
            if kind == "v_rest":
                return both(lambda hl: v_rest[:, hl, :], bank[:, 0:HALF], VF)
            if kind == "vip":
                step = NHN + HG * NIP
                for b in range(B):
                    for j in range(HG):
                        q = slice(D * j, D * j + D)
                        dst = vip_blk[q, b, :].rearrange("p (g r) -> p g r", r=step)
                        src = bank[q, 0:CC * B * NIP].rearrange("p (g n) -> p g n", g=CC)
                        last = plain(dst[:, :, j * NIP:(j + 1) * NIP], src[:, :, b * NIP:(b + 1) * NIP])
                return last
            assert kind == "wv"
            return both(lambda hl: wv_hl[:, hl, a, h * HALF:(h + 1) * HALF], bank[:, 0:HALF], WVF)

        def stack_ip_keys(hl, copy):
            for j in range(HG):
                for k in (hl, 2 + hl):
                    last = copy(k_tab[32 * k:32 * k + 32, j, :, :, T:TA],
                                k_nat[32 * j:32 * j + 32, hl, :, :, T:TA])
            return last

        FACTORS = {"kT": 1, "v": 2, "v_rest": 2, "kip": 5, "g": 1, "g_rest": 1, "wv": 6}
        Q_COLS = (slice(0, 4 * P), slice(4 * P, C))
        X_UP, Q_DOWN, P_UP = 2.0 ** 10, 2.0 ** -8, 2.0 ** 14

        @block.scalar
        def _(act):
            def copy(o, i, scale=1.0):
                return nc.scalar.activation(o, i, ACT.Copy, scale=scale)

            def row_squares(n, u):
                act.wait_ge(ld_x[u], (n - u + 2) * 8)
                if not before(n, 1):
                    act.wait_ge(xsq_guard, n)
                nc.scalar.activation(x_junk, x_in[:, u, :], ACT.Square, accum_out=x_sq[:, u:u + 1]
                                     ).then_inc(xsq_ready, 1)

            def x_high(n):
                act.wait_ge(xT_psum, n + 1)
                if not before(n, 1):
                    act.wait_ge(q_psum[1], n)
                copy(xT[:, HI], ps_m[:, 0:C].rearrange("p (c s) -> p c s", c=CC), X_UP
                     ).then_inc(xT_hi, 1)

            def q_high(n, u, bank):
                act.wait_ge(q_psum[bank], n + 1)
                if not before(n, 1):
                    act.wait_ge(ld_qs[1 - u], (n + u) * 128)
                copy(q_hl[:, HI, Q_COLS[bank]], ps_m[:, Q_COLS[bank]], Q_DOWN).then_inc(q_hi[bank], 1)

            def split_weight(loaded, dst, src, factors, f):
                act.wait_ge(loaded, 16)
                act.wait_ge(fac_ready, factors)
                copy(dst, src, F(f)).then_inc(wsplit_hi, 1)

            for k in range(len(jobs)):
                kind, who = jobs[k][0], jobs[k][3]
                if k == job_at("v")[1]:
                    split_weight(ld_q, wq_hl[:, HI], wq_sb, 3, WQF)
                if k == job_at("v")[3]:
                    split_weight(ld_out, wo_hl[:, HI], wo_sb, 4, WOF)
                if k == job_at("v")[0]:
                    inputs_read(act)
                    for n in range(2):
                        row_squares(n, n)
                if k == job_at("wv")[0]:
                    act.wait_ge(zeroed, 1)
                    emptied(act, job_at("v_rest")[0])
                    for hl in range(2):
                        for b in range(B):
                            for h in range(2):
                                r = slice(64 * h + 32 * b, 64 * h + 32 * b + TR)
                                vr = v_rest[r, hl, :].rearrange("p (n h d) -> p n h d", h=2, d=D)
                                for q in range(4):
                                    rows = slice(32 * q, 32 * q + TR)
                                    pairs = slice(h * NPR // 2, (h + 1) * NPR // 2)
                                    last = copy(t_rest[rows, hl, b, pairs, q % 2, 0:D], vr[:, :, q % 2, :])
                    last.then_inc(tables_ready, 1)
                if k in BESIDE:
                    what, n = BESIDE[k]
                    if what == "x":
                        x_high(n)
                    else:
                        q_high(n, n, 0)
                        q_high(n, n, 1)
                if who == "dve":
                    continue
                act.wait_ge(job_done, k + 1)
                if kind in FACTORS:
                    act.wait_ge(fac_ready, FACTORS[kind])
                if kind == "mask":
                    emptied(act, job_at("kip")[0])
                    act.wait_ge(job_act, by_act(job_at("kip")[0]))
                    stack_ip_keys(HI, copy).then_inc(ip_stacked, 1)
                if kind == "vip":
                    act.wait_ge(zeroed, 2)
                empty(k, copy, None, copy).then_inc(job_act, 1)
            prepared(act)

            def e_high(i, par):
                act.wait_ge(eT_psum, i + 1)
                if not (known(i) and i < 2):
                    act.wait_ge(prod, i - 1)
                copy(eT[:, par, HI, :], ps[:, BANK_T, :], P_UP).then_inc(eT_hi, 1)

            def copy_rest(i, par):
                act.wait_ge(rT_psum, i + 1)
                copy(rT[:, par].rearrange("p a s -> p (a s)"),
                     ps[:, BANK_T + 1, 0:P].bitcast(F16)).then_inc(rT_ready, 1)

            def copy_stats(i, g, u):
                act.wait_ge(dots, i + 1)
                src = ps[:, BANK_N:BANK_N + 2, 0:2 * W].rearrange("p b (h w) -> p b h w", h=2)
                dst = stats[:, u, g * HG:(g + 1) * HG, :].rearrange("p (b h) w -> p b h w", b=2)
                copy(dst, src[:, :, :, 0:W_G]).then_inc(stats_ready, 1)

            def exps(i, par, g, u, queries_of=None):
                act.wait_ge(max_ready, i + 1)
                src = ps[:, BANK_B:BANK_B + 2, 0:2 * TA].rearrange("p b (h t) -> p b h t", h=2)
                copy(ip_score[:, u, g * HG:(g + 1) * HG, :].rearrange("p (b h) n -> p b h n", b=2),
                     src[:, :, :, T:TA], row_ip[:, u:u + 1]).then_inc(ip_ready, 1)
                act.wait_ge(bias_ready, i + 1)
                if not (known(i) and i < NG):
                    act.wait_ge(dots, i - NG + 1)
                for j in range(HG):
                    src = ps[:, BANK_B + j // 2, (j % 2) * TA:(j % 2) * TA + T]
                    last = nc.scalar.activation(e[:, g, j, :], src, ACT.Exp, bias=s_bias[:, par, j:j + 1],
                                                scale=row_c[:, u:u + 1])
                    if j == 0 and queries_of:
                        q_high(*queries_of, 1)
                last.then_inc(e_ready, 1)

            def exp_ip(n):
                act.wait_ge(diff_ready, n + 1)
                nc.scalar.activation(e_ip, f_diff, ACT.Exp).then_inc(eip_ready, 1)

            def out_high(n):
                act.wait_ge(oT_psum, n + 1)
                if not before(n, 1):
                    act.wait_ge(y_psum, 2 * n)
                copy(oT[:, HI], ps_m[:, 0:C + P].rearrange("p (c s) -> p c s", c=CC + 1)
                     ).then_inc(oT_hi, 1)

            exps(0, 0, 0, 0)
            for n, u, _b, _f in tiles(act):
                for g in range(NG):
                    i = n * NG + g
                    par = (u * NG + g) % 2
                    if g == 0 and not before(n, 1) and not (known(n) and n + 1 >= NT):
                        q_high(n + 1, 1 - u, 0)
                    if g == 4 and loads_ahead(n):
                        x_high(n + 2)
                    e_high(i, par)
                    if not (known(i) and i == NT * NG - 1):
                        beside = g == 0 and not before(n, 1) and not (known(n) and n + 1 >= NT)
                        exps(i + 1, 1 - par, (g + 1) % NG, u if g < NG - 1 else 1 - u,
                             (n + 1, 1 - u) if beside else None)
                    copy_rest(i, par)
                    if not (known(i) and i < 1):
                        copy_stats(i - 1, (g - 1) % NG, u if g >= 1 else 1 - u)
                    if g == 0 and not before(n, 2):
                        out_high(n - 2)
                    if g == 1 and loads_ahead(n):
                        row_squares(n + 2, u)
                    if g == (3 if known(n) and n + 1 >= NT else 4) and not before(n, 1):
                        exp_ip(n - 1)
            out_high(NT - 2)
            copy_stats(NT * NG - 1, NG - 1, 1)
            exp_ip(NT - 1)
            out_high(NT - 1)

        @block.vector
        def _(dve):
            def ts(o, i, s1, s2=None, op0=ALU.mult, op1=None):
                if s2 is None:
                    return nc.vector.tensor_scalar(o, i, s1, None, op0)
                return nc.vector.tensor_scalar(o, i, s1, s2, op0, op1 or ALU.mult)

            def low_part(o, i, f, high):
                return nc.vector.scalar_tensor_tensor(out=o, in0=i, scalar=f, in1=high, op0=ALU.mult,
                                                      op1=ALU.subtract)

            links = [0]

            def link(ins):
                links[0] += 1
                ins.then_inc(fac_link, 1)
                dve.wait_ge(fac_link, links[0])

            def largest(dst, src):
                return nc.vector.tensor_reduce(dst, src, axis=AX_X, op=ALU.max, apply_absolute_value=True)

            def magnitude(m, k, src, r):
                if src is not None:
                    flat = src.rearrange("p a n -> p (a n)")
                    largest(N(M0 + m), flat).then_inc(part_max, 1)
                dve.wait_ge(all_max, k + 1)
                link(ts(N(m), N(m), 1e-15, op0=ALU.max))
                link(nc.vector.reciprocal(F(r), N(m)))

            dve.wait_ge(ld_ip, 16 * B)
            nc.vector.tensor_tensor_reduce(out=ip_nrm, in0=ip_raw, in1=ip_raw, scale=1.0,
                                           scalar=0.0, op0=ALU.mult, op1=ALU.add,
                                           accum_out=ip_sq).then_inc(ip_sq_ready, 1)
            dve.wait_ge(ip_sq_ready, 1)
            ts(ip_sqg, ip_sq, EPS * EPS, op0=ALU.max).then_inc(ip_guard, 1)
            link(nc.vector.memset(fac[:, SCR0:SCR2 + 1], 0.0))
            dve.wait_ge(ip_rn_ready, 1)
            ts(ip_nrm, ip_raw, ip_rn).then_inc(ip_nrm_ready, 1)
            dve.wait_ge(ld_ctx, 32 * B)
            link(largest(fac[0:P, SCR0:SCR0 + 1], ctx_main.rearrange("p a n -> p (a n)")))
            link(largest(fac[0:B * 32, SCR1:SCR1 + 1], ctx_rest))
            link(largest(fac[0:B * NIP, SCR2:SCR2 + 1], ip_raw))
            largest(N(M0 + N_CTX), fac[:, SCR0:SCR2 + 1]).then_inc(part_max, 1)

            def factors(kind):
                if kind == "kT":
                    magnitude(N_CTX, 0, None, R_CTX)
                    link(ts(F(AF), F(R_CTX), 2.0 ** 9))
                    link(ts(F(GF), F(R_CTX), F(R_CTX)))
                    link(ts(F(GSC), F(GF), EPS * EPS * 2.0 ** -10))
                    link(ts(F(GSC), F(GSC), 1e-37, op0=ALU.max))
                    link(ts(F(G2F), F(GF), 2.0 ** 5))
                    link(ts(F(GF), F(GF), 2.0 ** 4))
                    dve.wait_ge(ld_k_head, 16)
                    dve.wait_ge(ld_k, 16)
                    magnitude(N_WK, 1, w_stage[:, 0], R_WK)
                    link(ts(F(KF), F(R_WK), F(R_CTX)))
                    ts(F(KF), F(KF), SCALE * 2.0 ** 4).then_inc(fac_ready, 1)
                elif kind == "v":
                    dve.wait_ge(ld_v, 16)
                    magnitude(N_WV, 2, w_stage[:, 1], R_WV)
                    link(ts(F(VF), F(R_WV), F(R_CTX)))
                    ts(F(VF), F(VF), 2.0 ** 4).then_inc(fac_ready, 1)
                elif kind == "wq":
                    dve.wait_ge(ld_q, 16)
                    magnitude(N_WQ, 3, wq_sb, R_WQ)
                    ts(F(WQF), F(R_WQ), 2.0 ** 8).then_inc(fac_ready, 1)
                elif kind == "wo":
                    dve.wait_ge(ld_out, 16)
                    magnitude(N_WO, 4, wo_sb, R_WO)
                    ts(F(WOF), F(R_WO), 2.0 ** 8).then_inc(fac_ready, 1)
                elif kind == "kip":
                    dve.wait_ge(ld_kip, 16)
                    magnitude(N_WKI, 5, w_stage[:, 0], R_WKI)
                    link(ts(F(KIF), F(R_WKI), F(R_CTX)))
                    link(ts(F(KIF), F(KIF), SCALE * 2.0 ** 4))
                    link(ts(F(SCR0), N(N_WQ), N(N_CTX)))
                    link(ts(F(SCR0), F(SCR0), 2.0 ** -14))
                    link(ts(F(C1), F(SCR0), N(N_WK)))
                    ts(F(C2), F(SCR0), N(N_WKI)).then_inc(fac_ready, 1)
                elif kind == "wv":
                    dve.wait_ge(ld_vip, 16)
                    magnitude(N_WVI, 6, w_stage[:, 1], R_WVI)
                    link(nc.vector.tensor_tensor(F(N_WVJ), N(N_WVI), N(N_WV), ALU.max))
                    link(nc.vector.reciprocal(F(R_WVJ), F(N_WVJ)))
                    link(ts(F(RHO), N(N_WV), F(R_WVJ)))
                    link(ts(F(SCR0), F(R_WVJ), F(R_CTX)))
                    link(ts(F(SCR0), F(SCR0), 2.0 ** -2))
                    link(ts(F(SCR1), F(N_WVJ), N(N_CTX)))
                    link(ts(F(SCR1), F(SCR1), 2.0 ** -12))
                    link(ts(F(YM), F(SCR1), N(N_WO)))
                    ts(F(WVF), F(SCR0), F(R_WO)).then_inc(fac_ready, 1)

            def row_factors(n, u):
                dve.wait_ge(xrn_ready, n + 1)
                if not before(n, 2):
                    dve.wait_ge(e_ready, (n - 1) * NG)
                nc.vector.reciprocal(row_n[:, u:u + 1], x_rn[:, u:u + 1]).then_inc(rown_ready, 1)
                dve.wait_ge(rown_ready, n + 1)
                ts(row_c[:, u:u + 1], row_n[:, u:u + 1], F(C1)).then_inc(rowc_ready, 1)
                ts(row_ip[:, u:u + 1], row_n[:, u:u + 1], F(C2)).then_inc(rowc_ready, 1)

            def x_low(n):
                dve.wait_ge(xT_hi, n + 1)
                low_part(xT[:, LO], ps_m[:, 0:C].rearrange("p (c s) -> p c s", c=CC), X_UP, xT[:, HI]
                         ).then_inc(xT_lo, 1)

            def q_low(n, bank):
                dve.wait_ge(q_hi[bank], n + 1)
                cols = Q_COLS[bank]
                low_part(q_hl[:, LO, cols], ps_m[:, cols], Q_DOWN, q_hl[:, HI, cols]).then_inc(q_lo[bank], 1)

            MEASURE = {job_at("kT")[0]: "kT", job_at("kT")[2]: "v", job_at("v")[0]: "wq",
                       job_at("v")[2]: "wo", job_at("kip")[0]: "kip", job_at("wv")[0]: "wv"}
            for k in range(len(jobs)):
                kind, who = jobs[k][0], jobs[k][3]
                if k in MEASURE:
                    factors(MEASURE[k])
                if k == job_at("v")[2]:
                    dve.wait_ge(wsplit_hi, 1)
                    dve.wait_ge(fac_ready, 3)
                    low_part(wq_hl[:, LO], wq_sb, F(WQF), wq_hl[:, HI]).then_inc(wsplit_lo, 1)
                if k == job_at("v_rest")[0]:
                    dve.wait_ge(wsplit_hi, 2)
                    dve.wait_ge(fac_ready, 4)
                    low_part(wo_hl[:, LO], wo_sb, F(WOF), wo_hl[:, HI]).then_inc(wsplit_lo, 1)
                if k in BESIDE:
                    what, n = BESIDE[k]
                    if what == "x":
                        x_low(n)
                    else:
                        q_low(n, 0)
                        q_low(n, 1)
                if kind == "mask":
                    for n in range(2):
                        row_factors(n, n)
                    dve.wait_ge(job_dve, by_dve(k))
                    stack_ip_keys(LO, nc.vector.tensor_copy).then_inc(ip_stacked, 1)
                    dve.wait_ge(zeroed, 6)
                    for hl in range(2):
                        for b in range(B):
                            last = nc.vector.tensor_copy(t_main[:, hl, b, :, D:W],
                                                         repeated(g_nat[:, hl, b:b + 1, 0:W - D], 1, HEADS))
                            for q in range(4):
                                rows, r = slice(32 * q, 32 * q + TR), slice(32 * b, 32 * b + TR)
                                last = nc.vector.tensor_copy(
                                    t_rest[rows, hl, b, :, q % 2, D:WR],
                                    repeated(g_rest[r, hl:hl + 1, 0:WR - D], 1, NPR))
                    last.then_inc(tables_ready, 1)
                if who == "act":
                    continue
                dve.wait_ge(job_done, k + 1)
                if who == "both":
                    dve.wait_ge(job_act, by_act(k))
                    dve.wait_ge(fac_ready, FACTORS[kind])
                empty(k, None, low_part, nc.vector.tensor_copy
                      ).then_inc(job_dve, 1)
            prepared(dve)

            def maxima(i, par, g, u):
                dve.wait_ge(scores, i + 1)
                src = ps[:, BANK_B:BANK_B + 2, 0:2 * TA].rearrange("p b (h t) -> p b h t", h=2)
                nc.vector.tensor_reduce(s_max[:, par, :].rearrange("p (b h) -> p b h", b=2),
                                        src[:, :, :, 0:T], axis=AX_X, op=ALU.max).then_inc(max_ready, 1)
                dve.wait_ge(max_ready, i + 1)
                ts(s_bias[:, par, :], s_max[:, par, :], row_c[:, u:u + 1], -1.0).then_inc(bias_ready, 1)

            def e_low(i, par):
                dve.wait_ge(eT_hi, i + 1)
                low_part(eT[:, par, LO, :], ps[:, BANK_T, :], P_UP, eT[:, par, HI, :]).then_inc(eT_lo, 1)

            def group_dots(i, g, u):
                dve.wait_ge(prod, i + 1)
                for j in range(HG):
                    lo = (j % 2) * W + W_G
                    last = nc.vector.tensor_tensor_reduce(
                        out=e[:, g, j, :], in0=ps[:, BANK_N + j // 2, lo:lo + T], in1=e[:, g, j, :],
                        scale=1.0, scalar=0.0, op0=ALU.mult, op1=ALU.add,
                        accum_out=ege[:, u, g * HG + j:g * HG + j + 1])
                last.then_inc(dots, 1)

            CH = 6

            def tail_a(n, u):
                z = stats[:, u, :, W_Z]
                dve.wait_ge(stats_ready, (n + 1) * NG)
                dve.wait_ge(ip_ready, (n + 1) * NG)
                if not before(n, 1):
                    dve.wait_ge(text_ready, n)
                nc.vector.tensor_tensor(z_sq, z, z, ALU.mult).then_inc(chain, 1)
                nc.vector.tensor_copy(ip_kept, ip_score[:, u]).then_inc(ip_kept_ready, 1)
                nc.vector.reciprocal(z_inv, z).then_inc(z_link, 1)
                dve.wait_ge(chain, n * CH + 1)
                dve.wait_ge(dots, (n + 1) * NG)
                nc.vector.scalar_tensor_tensor(out=n_sq, in0=z_sq, scalar=F(GSC), in1=ege[:, u, :],
                                               op0=ALU.mult, op1=ALU.max).then_inc(nsq_ready, 1)
                dve.wait_ge(z_link, n + 1)
                ts(z_rho, z_inv, F(RHO)).then_inc(z_ready, 1)

            def tail_b(n, u):
                dve.wait_ge(ninv_ready, 2 * n + 2)
                nc.vector.tensor_tensor(sem_raw, stats[:, u, :, W_A:W_Z],
                                        repeated(n_inv.rearrange("p (h a) -> p h a", a=1), 2, NIP), ALU.mult
                                        ).then_inc(chain, 1)
                dve.wait_ge(chain, n * CH + 2)
                dve.wait_ge(ip_kept_ready, n + 1)
                nc.vector.scalar_tensor_tensor(out=fused, in0=sem_raw, scalar=SEM_SCALE * 2.0 ** -14,
                                               in1=ip_kept, op0=ALU.mult, op1=ALU.add
                                               ).then_inc(chain, 1)
                dve.wait_ge(chain, n * CH + 3)
                nc.vector.tensor_reduce(f_max, fused, axis=AX_X, op=ALU.max).then_inc(chain, 1)
                dve.wait_ge(chain, n * CH + 4)
                nc.vector.tensor_tensor(f_diff, fused, repeated(f_max.rearrange("p (h a) -> p h a", a=1), 2, NIP),
                                        ALU.subtract).then_inc(diff_ready, 1)

            def tail_c(n, col):
                dve.wait_ge(eip_ready, n + 1)
                nc.vector.reduce_sum(ip_sum, e_ip, AX_X).then_inc(chain, 1)
                dve.wait_ge(chain, n * CH + 5)
                nc.vector.reciprocal(ip_inv, ip_sum).then_inc(chain, 1)
                dve.wait_ge(chain, n * CH + 6)
                ts(ip_w, ip_inv, mask_sb[:, col], P_UP).then_inc(ipw_ready, 1)
                dve.wait_ge(ipw_ready, n + 1)
                if not before(n, 1):
                    dve.wait_ge(oT_psum, n)
                nc.vector.tensor_tensor(
                    p_ip[:, 0:NHN].rearrange("p (h n) -> p h n", n=NIP), e_ip,
                    repeated(ip_w.rearrange("p (h a) -> p h a", a=1), 2, NIP), ALU.mult
                ).then_inc(pip_ready, 1)

            def out_low(n):
                dve.wait_ge(oT_hi, n + 1)
                nc.vector.tensor_tensor(oT[:, LO], ps_m[:, 0:C + P].rearrange("p (c s) -> p c s", c=CC + 1),
                                        oT[:, HI], ALU.subtract).then_inc(oT_lo, 1)

            def add_residual(n, u, half):
                cols = slice(half * HALF, (half + 1) * HALF)
                dve.wait_ge(y_psum, 2 * n + half + 1)
                dve.wait_ge(res_ready, n + 1)
                if not before(n, 2):
                    dve.wait_ge(st_y[u], (n - u) * 8)
                nc.vector.scalar_tensor_tensor(
                    out=y[:, u, cols], in0=ps[:, BANK_M + half, 0:HALF], scalar=F(YM),
                    in1=x_res[:, u, cols], op0=ALU.mult, op1=ALU.add).then_inc(y_ready[half], 1)

            dve.wait_ge(pip_zero, 1)
            dve.wait_ge(rowc_ready, 4)
            maxima(0, 0, 0, 0)
            for n, u, b, _f in tiles(dve):
                for g in range(NG):
                    i = n * NG + g
                    par = (u * NG + g) % 2
                    if not (known(i) and i == NT * NG - 1):
                        if g == NG - 1:
                            dve.wait_ge(rowc_ready, 2 * n + 4)
                        maxima(i + 1, 1 - par, (g + 1) % NG, u if g < NG - 1 else 1 - u)
                    if g == 0 and not before(n, 1) and not (known(n) and n + 1 >= NT):
                        q_low(n + 1, 0)
                    if g == 1 and not before(n, 2):
                        out_low(n - 2)
                    if g == 4 and loads_ahead(n):
                        x_low(n + 2)
                    e_low(i, par)
                    if g == 0 and not before(n, 1) and not (known(n) and n + 1 >= NT):
                        q_low(n + 1, 1)
                    if g in (2, 3) and not before(n, 2):
                        add_residual(n - 2, u, g - 2)
                    if not (known(i) and i < 1):
                        group_dots(i - 1, (g - 1) % NG, u if g >= 1 else 1 - u)
                    if g == 1 and not before(n, 1):
                        tail_a(n - 1, 1 - u)
                    last_tile = known(n) and n + 1 >= NT
                    tail_step = 3 if last_tile else 4
                    if g == tail_step and not before(n, 1):
                        tail_b(n - 1, 1 - u)
                    if g == 4 and loads_ahead(n):
                        row_factors(n + 2, u)
                    if g == tail_step and not before(n, 1):
                        within = (n - 1) % TPB if known(n) else n - 1 - b * TPB
                        tail_c(n - 1, bass.ds(within, 1))
            n = NT - 1
            out_low(n - 1)
            group_dots(NT * NG - 1, NG - 1, 1)
            tail_a(n, 1)
            add_residual(n - 1, 0, 0)
            add_residual(n - 1, 0, 1)
            tail_b(n, 1)
            tail_c(n, bass.ds(TPB - 1, 1))
            out_low(n)
            add_residual(n, 1, 0)
            add_residual(n, 1, 1)

        PASSES = ((HI, HI), (HI, LO), (LO, HI))

        @block.tensor
        def _(pe):
            pe.wait_ge(ident_ready, 2)
            pe.wait_ge(ld_ctx, 32 * B)

            def run_job(k, chunks=range(EC)):
                kind, a, h, _ = jobs[k]
                bank = ps[:, k % 4, :]
                if k >= 4 and 0 in chunks:
                    emptied(pe, k - 4)
                if kind == "ctxT":
                    if k == 0:
                        pe.wait_ge(ip_nrm_ready, 1)
                    cols = slice(a * P, (a + 1) * P)
                    by_batch = bank[:, 0:C_IP].rearrange("p (b w) -> p b w", b=B)
                    parts = [(ctx_main[:, b, cols], by_batch[:, b, 0:P]) for b in range(B)]
                    parts += [(ctx_rest[:, cols], by_batch[:, :, C_REST:C_IPN]),
                              (ip_nrm[:, cols], by_batch[:, :, C_IPN:C_B]), (ip_raw[:, cols], bank[:, C_IP:C_ALL])]
                    for src, dst in parts:
                        n = src.shape[0]
                        last = nc.tensor.transpose(dst, src, ident[0:n, 0:n])
                    return last
                if kind == "mask":
                    pe.wait_ge(ld_small, 32)
                    return nc.tensor.transpose(bank[:, 0:TPB], mask_rows, ident[0:TPB, 0:TPB])
                if kind == "wv":
                    pe.wait_ge(ld_out, 16)
                    emptied(pe, job_at("vip")[0])
                    for q, c in [(c // 2, c) for c in range(CC)] + [(3, 0)]:
                        col = c * NHN + 32 * q
                        last = nc.tensor.matmul(bank[32 * q:32 * q + 32, 0:HALF], vip_blk[:, a, col:col + 32],
                                                wo_sb[:, c, h * HALF:(h + 1) * HALF],
                                                start=(c % 2 == 0), stop=(q >= 2 or c % 2 == 1),
                                                skip_group_check=True)
                    return last
                if k == job_at("kT")[0] and 0 in chunks:
                    for c in range(EC):
                        emptied(pe, c)
                load = {"kT": ld_k_head, "kip_part": ld_kip, "vip_part": ld_vip, "v": ld_v,
                        "v_rest": ld_v}.get(kind)
                if load and 0 in chunks:
                    pe.wait_ge(load, 16)
                if kind in ("kip", "vip"):
                    emptied(pe, k - 1)
                    pe.wait_ge(pick_ready, 5)
                    for g in range(CC):
                        last = nc.tensor.matmul(bank[:, g * B * NIP:(g + 1) * B * NIP],
                                                ip_parts[:, g * P:(g + 1) * P], ip_pick[:],
                                                start=(g == 0), stop=True, skip_group_check=True)
                    return last
                if kind in ("kip_part", "vip_part"):
                    if kind == "vip_part":
                        pe.wait_ge(job_done, job_at("kip")[0] + 1)
                    slot = 0 if kind == "kip_part" else 1
                    for c in range(EC):
                        q = c % 4
                        last = nc.tensor.matmul(
                            bank[32 * q:32 * q + 32, 0:HALF], ctxT[:, c, C_ALL - 32:C_ALL],
                            w_stage[:, slot, c, a * HALF:(a + 1) * HALF],
                            start=(c < 4), stop=(c >= EC - 4), skip_group_check=True)
                    return last
                if kind == "v_rest":
                    for c in range(EC):
                        for q in range(4):
                            half, b = q // 2, q % 2
                            last = nc.tensor.matmul(
                                bank[32 * q:32 * q + 32, 0:HALF],
                                ctxT[:, c, b * C_B + C_REST:b * C_B + C_IPN],
                                w_stage[:, 1, c, half * HALF:(half + 1) * HALF],
                                start=(c == 0), stop=(c == EC - 1), skip_group_check=True)
                    return last
                if kind == "g_rest":
                    for c in range(EC):
                        for b in range(B):
                            last = nc.tensor.matmul(
                                bank[32 * b:32 * b + 32, 0:C_B - C_REST],
                                ctxT[:, c, b * C_B + C_REST:b * C_B + C_IPN],
                                ctxT[:, c, b * C_B + C_REST:(b + 1) * C_B],
                                start=(c == 0), stop=(c == EC - 1), skip_group_check=True)
                    return last
                if kind == "kT" and EC - 1 in chunks:
                    pe.wait_ge(ld_k, 16)
                for c in chunks:
                    first, stop = c == 0, c == EC - 1
                    if kind == "kT":
                        last = nc.tensor.matmul(
                            bank[:, 0:B * C_IPN], w_stage[:, 0, c, a * P:(a + 1) * P],
                            ctxT[:, c, 0:C_IP].rearrange("p (b w) -> p b w", b=B)[:, :, 0:C_IPN],
                            start=first, stop=stop)
                    elif kind == "g":
                        last = nc.tensor.matmul(bank[:, 0:C_B], ctxT[:, c, a * C_B:a * C_B + P],
                                                ctxT[:, c, a * C_B:(a + 1) * C_B], start=first, stop=stop)
                    else:
                        assert kind == "v"
                        last = nc.tensor.matmul(bank[:, 0:HALF], ctxT[:, c, a * C_B:a * C_B + P],
                                                w_stage[:, 1, c, h * HALF:(h + 1) * HALF],
                                                start=first, stop=stop)
                return last

            def transpose_x(n):
                pe.wait_ge(xhat_ready, n + 1)
                for c in range(CC):
                    last = nc.tensor.transpose(ps_m[:, c * P:(c + 1) * P], x_hat[:, c * P:(c + 1) * P], ident[:])
                last.then_inc(xT_psum, 1)

            def queries(n, chunks):
                if 0 in chunks:
                    pe.wait_ge(xT_lo, n + 1)
                for k in chunks:
                    for w_part, x_part in PASSES:
                        for c in range(CC):
                            first = (w_part, x_part) == PASSES[0] and c == 0
                            final = (w_part, x_part) == PASSES[-1] and c == CC - 1
                            last = nc.tensor.matmul(
                                ps_m[:, k * P:(k + 1) * P], wq_hl[:, w_part, c, k * P:(k + 1) * P],
                                xT[:, x_part, c, :], start=(first and k in (0, 4)), stop=final,
                                skip_group_check=True)
                    if k == 3:
                        last.then_inc(q_psum[0], 1)
                if chunks[-1] == CC - 1:
                    last.then_inc(q_psum[1], 1)

            def group_scores(i, g, u, b):
                for j in range(HG):
                    last = nc.tensor.matmul(ps[:, BANK_B + j // 2, (j % 2) * TA:(j % 2 + 1) * TA],
                                            q_stack[:, u, j, g * P:(g + 1) * P], k_tab[:, j, b, g, :],
                                            start=(j % 2 == 0), stop=True, skip_group_check=True)
                last.then_inc(scores, 1)

            def transpose_out(n, queries_out=None):
                pe.wait_ge(text_ready, n + 1)
                pe.wait_ge(pip_ready, n + 1)
                for c in range(CC):
                    if c == 4 and queries_out is not None:
                        pe.wait_ge(q_lo[1], queries_out)
                    nc.tensor.transpose(ps_m[:, c * P:(c + 1) * P], text[:, c * HG:(c + 1) * HG, :], ident[:])
                nc.tensor.transpose(ps_m[:, C:C + P], p_ip, ident[:]).then_inc(oT_psum, 1)

            def output_product(n, h, b, passes=PASSES):
                cols = slice(h * HALF, (h + 1) * HALF)
                dst = ps[:, BANK_M + h, 0:HALF]
                for o_part, w_part in passes:
                    if h == 0 and (o_part, w_part) == PASSES[0]:
                        pe.wait_ge(oT_lo, n + 1)
                    for c in range(CC):
                        nc.tensor.matmul(dst, oT[:, o_part, c, :], wo_hl[:, w_part, c, cols],
                                         start=((o_part, w_part) == PASSES[0] and c == 0), stop=False)
                    last = nc.tensor.matmul(dst, oT[:, o_part, CC, :], wv_hl[:, w_part, b, cols],
                                            start=False, stop=((o_part, w_part) == PASSES[-1]))
                if passes[-1] == PASSES[-1]:
                    last.then_inc(y_psum, 1)

            def main_product(i, par, g, b):
                pe.wait_ge(eT_hi, i + 1)
                pe.wait_ge(rT_ready, i + 1)
                if not (known(i) and i < 1):
                    pe.wait_ge(stats_ready, i)
                for pr in range(2):
                    for e_part, t_part in PASSES:
                        if pr == 0 and e_part == LO:
                            pe.wait_ge(eT_lo, i + 1)
                        for hh in range(2):
                            j = 2 * pr + hh
                            nc.tensor.matmul(ps[:, BANK_N + pr, hh * W:(hh + 1) * W],
                                             eT[:, par, e_part, j * P:(j + 1) * P],
                                             t_main[:, t_part, b, g * HG + j, :],
                                             start=(hh == 0 and (e_part, t_part) == PASSES[0]), stop=False,
                                             skip_group_check=True)
                    dst = ps[:, BANK_N + pr, 0:2 * W].rearrange("p (h w) -> p h w", h=2)[:, :, 0:WR]
                    for t_part in range(2):
                        last = nc.tensor.matmul(dst, rT[:, par, pr, :], t_rest[:, t_part, b, 2 * g + pr],
                                                start=False, stop=(t_part == 1), skip_group_check=True)
                last.then_inc(prod, 1)

            def transpose_main(i, g):
                if not (known(i) and i < 1):
                    pe.wait_ge(eT_lo, i)
                for j in range(HG):
                    last = nc.tensor.transpose(ps[:, BANK_T, j * P:(j + 1) * P], e[:, g, j, TR:T], ident[:])
                last.then_inc(eT_psum, 1)

            def transpose_rest(i):
                pe.wait_ge(rest_lo, i + 1)
                for pr in range(2):
                    last = nc.tensor.transpose(
                        ps[:, BANK_T + 1, pr * P // 2:(pr + 1) * P // 2].bitcast(F16),
                        e_rest[:, pr].rearrange("p a h t -> p (a h t)"), ident16[:])
                last.then_inc(rT_psum, 1)

            for k in range(len(jobs)):
                if k in BESIDE:
                    what, n = BESIDE[k]
                    if what == "x":
                        if n:
                            pe.wait_ge(q_lo[0], n)
                            pe.wait_ge(q_lo[1], n)
                        transpose_x(n)
                    else:
                        pe.wait_ge(wsplit_lo, 1)
                        queries(n, range(CC))
                if k == job_at("kT")[0]:
                    for early in job_at("kT")[:4]:
                        run_job(early, range(EC // 2))
                if k in job_at("kT")[:4]:
                    last = run_job(k, range(EC // 2, EC))
                else:
                    last = run_job(k)
                last.then_inc(job_done, 1)
            prepared(pe)
            pe.wait_ge(ld_qs[0], 256)
            group_scores(0, 0, 0, 0)
            for n, u, b, first_pair in tiles(pe):
                for g in range(NG):
                    i = n * NG + g
                    par = (u * NG + g) % 2
                    pe.wait_ge(ip_ready, i + 1)
                    pe.wait_ge(e_ready, i + 1)
                    if not (known(i) and i == NT * NG - 1):
                        nb = b
                        if g == NG - 1:
                            pe.wait_ge(ld_qs[1 - u], (n + u + 2) * 128)
                            if known(n):
                                nb = (n + 1) // TPB
                        group_scores(i + 1, (g + 1) % NG, u if g < NG - 1 else 1 - u, nb)
                    transpose_main(i, g)
                    if g == 0 and not before(n, 1) and not (known(n) and n + 1 >= NT):
                        queries(n + 1, (4,))
                    out_b = b - 1 if first_pair and b else b
                    if g == 3 and not before(n, 2):
                        output_product(n - 2, 1, out_b, PASSES[2:])
                    if not (known(i) and i < 1):
                        pb = b - 1 if first_pair and b and u == 0 and g == 0 else b
                        main_product(i - 1, 1 - par, (g - 1) % NG, pb)
                    transpose_rest(i)
                    if g == 0 and not before(n, 2):
                        if known(n) and n + 1 >= NT:
                            residual_added(pe, n - 2)
                        else:
                            pe.wait_ge(q_lo[0], n + 2)
                        last_tile = known(n) and n + 1 >= NT
                        transpose_out(n - 2, None if last_tile else n + 2)
                    if g in (1, 2) and not before(n, 2):
                        output_product(n - 2, g - 1, out_b, PASSES if g == 1 else PASSES[:2])
                    if g == 3 and loads_ahead(n):
                        if not before(n, 2):
                            residual_added(pe, n - 1)
                        else:
                            pe.wait_ge(q_lo[0], n + 2)
                            pe.wait_ge(q_lo[1], n + 2)
                        transpose_x(n + 2)
                    if g == 4 and loads_ahead(n):
                        queries(n + 2, range(4))
            for n in (NT - 2, NT - 1):
                residual_added(pe, n)
                transpose_out(n)
                if n == NT - 2:
                    main_product(NT * NG - 1, 1, NG - 1, B - 1)
                output_product(n, 0, B - 1)
                output_product(n, 1, B - 1)


_INS = ["x", "ctx_2048", "fside_S_0", "L0_xattn_W_q", "L0_xattn_W_k", "L0_xattn_W_v",
        "L0_xattn_W_k_ip", "L0_xattn_W_v_ip", "L0_xattn_W_out", "L0_xattn_b_out"]


def kernel(**inputs):
    import numpy as np
    import concourse.bacc as bacc
    from concourse.bass_utils import run_bass_kernel_spmd

    nc = bacc.Bacc("TRN2", target_bir_lowering=False, num_devices=1)
    arrays, args = {}, []
    for name in _INS:
        a = np.ascontiguousarray(inputs[name])
        arrays[f"in_{name}"] = a
        args.append(nc.dram_tensor(f"in_{name}", a.shape, mybir.dt.from_np(a.dtype),
                                   kind="ExternalInput").ap())
    shape = tuple(inputs["x"].shape)
    out = nc.dram_tensor("out", shape, F32, kind="ExternalOutput").ap()
    xattn_program(nc, *args, out)
    got = run_bass_kernel_spmd(nc, [arrays], core_ids=[0])
    return got.results[0]["out"]
```
